# Optimizing a Trainium2 kernel written in Bass

```python
import numpy as np
import jax
import jax.numpy as jnp

def _softmax(x, axis=-1):
    return jax.nn.softmax(x, axis=axis)

def _gelu(x):
    return jax.nn.gelu(x, approximate=True)

def _silu(x):
    return jax.nn.silu(x)

def _sigmoid(x):
    return jax.nn.sigmoid(x)

def _layernorm(x, axis=-1, eps=1e-05):
    m = jnp.mean(x, axis=axis, keepdims=True)
    v = jnp.var(x, axis=axis, keepdims=True)
    return (x - m) / jnp.sqrt(v + eps)

def _scatter_add(tgt, idx, src, axis=0):
    return tgt.at[idx].add(src)

def _segment_sum(src, seg, n):
    return jax.ops.segment_sum(src, seg, n)
kernel_name = 'mk_xattn_ffn_d1_seqx_r4_5a5a89'

def setup_inputs(seed: int=0):
    np.random.seed(seed)
    _w = jnp.asarray

    def _rec_inputs():
        import jax
        import jax.numpy as jnp
        _rk = jax.random.key(seed)
        x = -0.0002928 + 1 * jax.random.normal(jax.random.fold_in(_rk, 1), (4, 512, 256), jnp.float32)
        _lenS = 512 - jax.random.randint(jax.random.fold_in(_rk, 7), (4,), 0, max(1, 512 // 4) + 1, jnp.int32)
        _lenS2 = 512 - jax.random.randint(jax.random.fold_in(_rk, 8), (4,), 0, max(1, 512 // 4) + 1, jnp.int32)
        _ctx_1024P = jax.random.normal(jax.random.fold_in(_rk, 11), (4, 16, 256), jnp.float32)
        _ctx_1024c = jax.random.dirichlet(jax.random.fold_in(_rk, 511), 0.3 * jnp.ones((16,), jnp.float32), (4, 512))
        _ctx_1024t = jnp.einsum('bsk,bkd->bsd', _ctx_1024c, _ctx_1024P)
        _ctx_1024t = _ctx_1024t * jax.lax.rsqrt(jnp.mean(jnp.square(_ctx_1024t)) + 1e-12) * 0.953939
        ctx_1024 = -1.39393e-06 + 0.999914 * (_ctx_1024t + 0.3 * jax.random.normal(jax.random.fold_in(_rk, 611), (4, 512, 256), jnp.float32))
        return (x, ctx_1024)
    x, ctx_1024 = _rec_inputs()

    def _L0_xattn_setup():
        import jax, jax.numpy as jnp
        import numpy as np
        D_MODEL = 256
        N_HEADS = 16
        D_HEAD = D_MODEL // N_HEADS
        WINDOW = 128

        def _heads(x):
            B, S, _ = x.shape
            return x.reshape(B, S, N_HEADS, D_HEAD).transpose(0, 2, 1, 3)
        key = jax.random.key(seed)
        ks = jax.random.split(key, 11)
        B, S = (1, 1024)
        s = 1.0 / np.sqrt(D_MODEL)
        return {'query': jax.random.normal(ks[0], (B, S, D_MODEL), jnp.float32), 'key': jax.random.normal(ks[1], (B, S, D_MODEL), jnp.float32), 'value': jax.random.normal(ks[2], (B, S, D_MODEL), jnp.float32), 'Wq': jax.random.normal(ks[3], (D_MODEL, D_MODEL), jnp.float32) * s, 'bq': jnp.zeros((D_MODEL,), jnp.float32), 'Wk': jax.random.normal(ks[4], (D_MODEL, D_MODEL), jnp.float32) * s, 'bk': jnp.zeros((D_MODEL,), jnp.float32), 'Wv': jax.random.normal(ks[5], (D_MODEL, D_MODEL), jnp.float32) * s, 'bv': jnp.zeros((D_MODEL,), jnp.float32), 'Wo': jax.random.normal(ks[6], (D_MODEL, D_MODEL), jnp.float32) * s, 'bo': jnp.zeros((D_MODEL,), jnp.float32)}
    _L0_xattn_all = _L0_xattn_setup()
    _L0_xattn_in = {k: v for k, v in _L0_xattn_all.items() if k in ('Wq', 'bq', 'Wk', 'bk', 'Wv', 'bv', 'Wo', 'bo')}
    del _L0_xattn_all

    def _L0_ffn_setup():
        import jax, jax.numpy as jnp
        import numpy as np

        def _binarize(w):
            alpha = jax.lax.stop_gradient(jnp.mean(jnp.abs(w), axis=1, keepdims=True))
            bw = alpha * jnp.sign(w)
            return w + jax.lax.stop_gradient(bw - w)
        key = jax.random.key(seed)
        k1, k2, k3, k4, k5 = jax.random.split(key, 5)
        D, H = (256, 1024)
        x = jax.random.normal(k1, (64, 196, D), dtype=jnp.float32)
        w1 = jax.random.normal(k2, (H, D), dtype=jnp.float32) * 0.02
        b1 = jax.random.normal(k3, (H,), dtype=jnp.float32) * 0.02
        w2 = jax.random.normal(k4, (D, H), dtype=jnp.float32) * 0.02
        b2 = jax.random.normal(k5, (D,), dtype=jnp.float32) * 0.02
        return {'x': x, 'w1': w1, 'b1': b1, 'w2': w2, 'b2': b2}
    _L0_ffn_all = _L0_ffn_setup()
    _L0_ffn_in = {k: v for k, v in _L0_ffn_all.items() if k in ('w1', 'b1', 'w2', 'b2')}
    del _L0_ffn_all
    return {'x': x, 'ctx_1024': ctx_1024, 'L0_xattn_Wq': _L0_xattn_in['Wq'], 'L0_xattn_bq': _L0_xattn_in['bq'], 'L0_xattn_Wk': _L0_xattn_in['Wk'], 'L0_xattn_bk': _L0_xattn_in['bk'], 'L0_xattn_Wv': _L0_xattn_in['Wv'], 'L0_xattn_bv': _L0_xattn_in['bv'], 'L0_xattn_Wo': _L0_xattn_in['Wo'], 'L0_xattn_bo': _L0_xattn_in['bo'], 'L0_ffn_w1': _L0_ffn_in['w1'], 'L0_ffn_b1': _L0_ffn_in['b1'], 'L0_ffn_w2': _L0_ffn_in['w2'], 'L0_ffn_b2': _L0_ffn_in['b2']}

def reference(x, ctx_1024, L0_xattn_Wq, L0_xattn_bq, L0_xattn_Wk, L0_xattn_bk, L0_xattn_Wv, L0_xattn_bv, L0_xattn_Wo, L0_xattn_bo, L0_ffn_w1, L0_ffn_b1, L0_ffn_w2, L0_ffn_b2):
    import jax
    import jax.numpy as jnp

    def _L0_xattn_ref(query, key, value, Wq, bq, Wk, bk, Wv, bv, Wo, bo):
        import jax, jax.numpy as jnp
        import numpy as np
        D_MODEL = 256
        N_HEADS = 16
        D_HEAD = D_MODEL // N_HEADS
        WINDOW = 128

        def _heads(x):
            B, S, _ = x.shape
            return x.reshape(B, S, N_HEADS, D_HEAD).transpose(0, 2, 1, 3)
        B, S, _ = query.shape
        q = _heads(query @ Wq.T + bq)
        k = _heads(key @ Wk.T + bk)
        v = _heads(value @ Wv.T + bv)
        scores = jnp.einsum('bhqd,bhkd->bhqk', q, k) / np.sqrt(D_HEAD).astype(np.float32)
        idx = jnp.arange(S)
        local = jnp.abs(idx[:, None] - idx[None, :]) <= WINDOW // 2
        scores = jnp.where(local[None, None, :, :], scores, -jnp.inf)
        attn = jax.nn.softmax(scores, axis=-1)
        ctx = jnp.einsum('bhqk,bhkd->bhqd', attn, v)
        ctx = ctx.transpose(0, 2, 1, 3).reshape(B, S, D_MODEL)
        return ctx @ Wo.T + bo

    def _L0_ffn_ref(x, w1, b1, w2, b2):
        import jax, jax.numpy as jnp
        import numpy as np

        def _binarize(w):
            alpha = jax.lax.stop_gradient(jnp.mean(jnp.abs(w), axis=1, keepdims=True))
            bw = alpha * jnp.sign(w)
            return w + jax.lax.stop_gradient(bw - w)
        bw1 = _binarize(w1)
        h = jnp.einsum('bsd,hd->bsh', x, bw1) + b1
        h = jax.nn.gelu(h, approximate=False)
        bw2 = _binarize(w2)
        out = jnp.einsum('bsh,dh->bsd', h, bw2) + b2
        return out
    x = x + _L0_xattn_ref(_layernorm(x, axis=-1), ctx_1024, ctx_1024, L0_xattn_Wq, L0_xattn_bq, L0_xattn_Wk, L0_xattn_bk, L0_xattn_Wv, L0_xattn_bv, L0_xattn_Wo, L0_xattn_bo)
    x = x + _L0_ffn_ref(_layernorm(x, axis=-1), L0_ffn_w1, L0_ffn_b1, L0_ffn_w2, L0_ffn_b2)
    return x

_drawn_inputs = setup_inputs


def setup_inputs(seed=0):
    import zlib

    import numpy as np

    out = dict(_drawn_inputs(seed))
    spreads = {'L0_xattn_bq': (0.0, 0.377),
     'L0_xattn_bk': (0.0, 0.8),
     'L0_xattn_bv': (0.0, 0.1),
     'L0_xattn_bo': (0.0, 0.1)}
    factors = {'L0_ffn_b1': 8.0, 'L0_ffn_b2': 3.376}
    for name, (base, spread) in spreads.items():
        noise = np.random.default_rng([zlib.crc32(name.encode()), seed]).standard_normal(out[name].shape)
        drawn = base * np.exp(spread * noise) if base else spread * noise
        out[name] = jnp.asarray(drawn.astype(out[name].dtype))
    for name, factor in factors.items():
        out[name] = (out[name] * factor).astype(out[name].dtype)
    return out
```

```python
from contextlib import ExitStack

import concourse.bass as bass
from concourse import mybir

ALU = mybir.AluOpType
ACT = mybir.ActivationFunctionType
AX = mybir.AxisListType
F32 = mybir.dt.float32
F32R = mybir.dt.float32r
BF16 = mybir.dt.bfloat16

P = 128
B, S, D = 4, 512, 256
H, DH = 16, 16
F = 1024
REACH = 64
EPS = 1e-5
BIG = 3.0e38

C = D // P
TT = S // P
FC = F // P
QB = 32
NB = S // QB
WB = 2 * REACH // QB + 1
WIN = WB * QB
UNITS = 4
HU = H // UNITS
PER_BANK = 3
NWIN = UNITS * NB
STEPS = -(-NWIN // PER_BANK)
AHEAD = 3
RING = 6
TPAD = REACH // QB
TJ = NB + 2 * TPAD
SCALE = DH ** -0.5

C_IDENT, C_QUAD, C_HEAD, C_DELTA, C_EDGE = 0, 128, 256, 264, 296
C_END = C_EDGE + 2 * QB


def windows_of(t):
    return [(n // NB, n % NB, n - PER_BANK * t)
            for n in range(PER_BANK * t, min(PER_BANK * (t + 1), NWIN))]


def runs_of(t):
    out = []
    for u, j, slot in windows_of(t):
        if out and out[-1][0] == u:
            out[-1][2] += 1
        else:
            out.append([u, j, 1, slot])
    return out


def finished_blocks(t):
    out = []
    for u, j, n, _ in runs_of(t):
        before = max(0, j - TPAD)
        after = NB if j + n == NB else max(0, j + n - TPAD)
        if after > before:
            out.append((u, before, after))
    return out


def last_step(u):
    return (NB * (u + 1) - 1) // PER_BANK


class Banks:

    def __init__(self, names):
        self.place, self.uses, turn = {}, [0] * 8, 0
        for name, bank in names:
            if bank is None:
                bank, turn = turn % RING, turn + 1
            self.place[name] = (bank, self.uses[bank])
            self.uses[bank] += 1


def bank_uses(prefetch, attention):
    names = []
    if attention:
        for t in range(STEPS + AHEAD + 1):
            if t < STEPS:
                names.append((("scores", t), None))
            for u in range(UNITS):
                if t - AHEAD - 1 == (NB * u) // PER_BANK:
                    names.append((("context", u), 6 + u % 2))
            if prefetch and t in T1_AT:
                names.append((("norm1_t", T1_AT.index(t)), None))
    elif prefetch:
        names += [(("norm1_t", c), None) for c in range(C)]
    if prefetch:
        names += [((kind, m), None) for kind in ("q", "k") for m in range(C)]
    if attention:
        names += [(("attn_out", i), None) for i in range(TT // 2)]
    if prefetch:
        names += [(("v", m), None) for m in range(C)]
    if attention:
        names += [(("norm2_t", c), None) for c in range(C)]
        names += [(("hidden", i), None) for i in range(FC)]
        names += [(("ffn_out", i), 6 + i) for i in range(2)]
    else:
        names += [("alpha1", 6), ("alpha2", 7)]
    return Banks(names)


DVE_OWN = 62
T1_AT = (12, 15)


def xattn_ffn_kernel(nc, x, ctx_t, wq_t, wk_t, wv_t, wo_t, w1_t, w2_t, cols, rows, consts, out):
    START, LOOP, LAST = bank_uses(True, False), bank_uses(True, True), bank_uses(False, True)

    with ExitStack() as ctx:
        def sb(name, shape, dt=F32):
            return ctx.enter_context(nc.sbuf_tensor(name, shape, dt))

        def sem(name):
            return ctx.enter_context(nc.semaphore(name))

        bank = [ctx.enter_context(nc.psum_tensor(f"bank{i}", [P, 512], F32)) for i in range(8)]

        wq = sb("wq", [P, C, D])
        wk = sb("wk", [P, C, D])
        wv = sb("wv", [P, C, D])
        wo = sb("wo", [P, C, D])
        raw = sb("raw", [P, 2 * C * F])
        w1 = raw[:, 0:C * F].rearrange("p (c n) -> p c n", c=C)
        w2 = raw[:, C * F:].rearrange("p (c n) -> p c n", c=FC)
        hid = raw[:, 0:3 * S].rearrange("p (i s) -> p i s", i=3)
        x1_b2 = raw[:, 3 * S:5 * S].rearrange("p (t d) -> p t d", t=TT)
        y = raw[:, 5 * S:7 * S].rearrange("p (t d) -> p t d", t=TT)
        sign1 = sb("sign1", [P, C, F], F32R)
        sign2 = sb("sign2", [P, FC, D], F32R)
        alpha1 = sb("alpha1", [P, FC])
        alpha2 = sb("alpha2", [P, D])
        col = sb("col", [P, 3 * C + FC])
        bo_row = sb("bo_row", [P, D])
        b2_row = sb("b2_row", [P, D])
        const = sb("const", [P, C_END])
        quad_ones = sb("quad_ones", [P, P], F32R)
        ident16 = sb("ident16", [P, P], BF16)
        edge16 = sb("edge16", [P, 2, QB], BF16)
        ones = sb("ones", [P, P])
        minus_half = sb("minus_half", [P, TT])
        eps = sb("eps", [P, TT])
        wait_slot = sb("wait_slot", [P, 1])
        ident = const[:, C_IDENT:C_IDENT + P]
        head_mask = const[:, C_HEAD:C_HEAD + 2 * HU]
        delta = const[:, C_DELTA:C_DELTA + QB]
        bq, bk, bv, b1 = col[:, 0:C], col[:, C:2 * C], col[:, 2 * C:3 * C], col[:, 3 * C:]

        x_in = sb("x_in", [P, TT, D])
        ctx_in = sb("ctx_in", [P, C, S])
        x_bo = sb("x_bo", [P, TT, D])
        stats1 = sb("stats1", [P, TT, 6])
        mv1 = sb("mv1", [P, TT, 2])
        rstd1 = sb("rstd1", [P, TT])
        norm1 = sb("norm1", [P, TT, D])
        norm1_t = sb("norm1_t", [P, C, S])
        q_t = sb("q_t", [P, C, S + 2 * REACH])
        k_t = sb("k_t", [P, C, S])
        v_t = sb("v_t", [P, C, S])
        k_diag = sb("k_diag", [P, UNITS, NB, P])
        v_ones = sb("v_ones", [P, UNITS, NB, P])

        part_max = sb("part_max", [P, 2, TJ, WB])
        neg_max = sb("neg_max", [P, 2, NB])
        max_diag = sb("max_diag", [P, 2, S + 2 * REACH], F32R)
        probs = sb("probs", [P, 3, PER_BANK, WIN])
        num = sb("num", [P, C, S])
        den = sb("den", [P, S])
        attn_t = sb("attn_t", [P, C, S])

        x1 = sb("x1", [P, TT, D])
        stats2 = sb("stats2", [P, TT, 6])
        mv2 = sb("mv2", [P, TT, 2])
        rstd2 = sb("rstd2", [P, TT])
        norm2 = sb("norm2", [P, TT, D])
        n2_hi = sb("n2_hi", [P, C, S], F32R)
        n2_lo = sb("n2_lo", [P, C, S], F32R)
        hid_hi = sb("hid_hi", [P, 3, S], F32R)
        hid_lo = sb("hid_lo", [P, 3, S], F32R)

        const_loaded = sem("const_loaded")
        x_loaded = sem("x_loaded")
        ctx_loaded = sem("ctx_loaded")
        wq_loaded, wk_loaded, wv_loaded = sem("wq_loaded"), sem("wk_loaded"), sem("wv_loaded")
        wo_loaded, w12_loaded = sem("wo_loaded"), sem("w12_loaded")
        y_free = sem("y_free")
        tables_ready = sem("tables_ready")
        zeros_ready = sem("zeros_ready")
        signs_ready = sem("signs_ready")
        abs_ready = sem("abs_ready")
        filled = [sem(f"filled{i}") for i in range(8)]
        emptied = [sem(f"emptied{i}") for i in range(8)]
        dve_done, pool_done = sem("dve_done"), sem("pool_done")
        stats1_ready, rstd1_ready, norm1_ready = sem("stats1_ready"), sem("rstd1_ready"), sem("norm1_ready")
        k_diag_dve, k_diag_pool, v_ready = sem("k_diag_dve"), sem("k_diag_pool"), sem("v_ready")
        x_bo_ready = sem("x_bo_ready")
        max_ready, shifted, probs_used = sem("max_ready"), sem("shifted"), sem("probs_used")
        ctx_raw_ready, attn_ready = sem("ctx_raw_ready"), sem("attn_ready")
        x1_b2_ready = sem("x1_b2_ready")
        stats2_ready, rstd2_ready, norm2_ready = sem("stats2_ready"), sem("rstd2_ready"), sem("norm2_ready")
        n2_hi_ready = sem("n2_hi_ready")
        hid_hi_ready, hid_lo_ready, hid_used = sem("hid_hi_ready"), sem("hid_lo_ready"), sem("hid_used")
        y_ready = sem("y_ready")

        def part(tile_ap, offset, *dims):
            return bass.AP(tile_ap.tensor, tile_ap.offset + offset, [tile_ap.ap[0], *dims])

        def uses_before(plan, b, name):
            i, n = plan.place[name]
            if plan is START:
                return i, n
            return i, b * LOOP.uses[i] + (START.uses[i] + n)

        def wait_filled(eng, plan, b, name):
            i, before = uses_before(plan, b, name)
            eng.wait_ge(filled[i], before + 1)
            return i

        def wait_read(eng, plan, b, name):
            i, before = uses_before(plan, b, name)
            eng.wait_ge(emptied[i], before + 1)

        class Own:

            def __init__(self, eng, done):
                self.eng, self.done, self.base, self.n = eng, done, 0, 0

            def mark(self, ins):
                self.n += 1
                return ins.then_inc(self.done, 1)

            def wait(self):
                self.eng.wait_ge(self.done, self.base + self.n)

            def enter(self, base):
                self.base, self.n = base, 0

        def tokens(dram, offset):
            return bass.AP(dram.tensor, offset, [[D, P], [P * D, TT], [1, D]])

        def features(dram, offset):
            return bass.AP(dram.tensor, offset, [[S, P], [P * S, C], [1, S]])

        block = ctx.enter_context(nc.Block())

        @block.sync
        def _(sp):
            sp.dma_start(x_in[:, :, :], tokens(x, 0)).then_inc(x_loaded, 16)
            sp.dma_start(const[:, :], consts).then_inc(const_loaded, 16)
            sp.dma_start(col[:, :], cols).then_inc(const_loaded, 16)
            sp.dma_start(wq[:, :, :], wq_t.rearrange("(c p) n -> p c n", p=P)).then_inc(wq_loaded, 16)
            sp.dma_start(ctx_in[:, :, :], features(ctx_t, 0)).then_inc(ctx_loaded, 16)
            sp.dma_start(wk[:, :, :], wk_t.rearrange("(c p) n -> p c n", p=P)).then_inc(wk_loaded, 16)
            sp.dma_start(wv[:, :, :], wv_t.rearrange("(c p) n -> p c n", p=P)).then_inc(wv_loaded, 16)
            sp.dma_start(bo_row[:, :], rows[0:1, :].partition_broadcast(P)).then_inc(const_loaded, 16)
            sp.dma_start(b2_row[:, :], rows[1:2, :].partition_broadcast(P)).then_inc(const_loaded, 16)
            sp.dma_start(w1[:, :, :], w1_t.rearrange("(c p) n -> p c n", p=P)).then_inc(w12_loaded, 16)
            sp.dma_start(w2[:, :, :], w2_t.rearrange("(c p) n -> p c n", p=P)).then_inc(w12_loaded, 16)
            sp.dma_start(wo[:, :, :], wo_t.rearrange("(c p) n -> p c n", p=P)).then_inc(wo_loaded, 16)

            with sp.Fori(0, B - 1) as b:
                next_row = sp.snap(b * (S * D) + S * D)
                rows_done, projected = sp.snap(b + 1), sp.snap(C * b + C)
                sp.wait_ge(x_bo_ready, rows_done)
                sp.wait_ge(norm1_ready, rows_done)
                sp.wait_ge(v_ready, projected)
                sp.dma_start(x_in[:, :, :], tokens(x, next_row)).then_inc(x_loaded, 16)
                sp.dma_start(ctx_in[:, :, :], features(ctx_t, next_row)).then_inc(ctx_loaded, 16)

        @block.gpsimd
        def _(pool):
            own = Own(pool, pool_done)

            def rstd(stats_ready, ready, mv, dst, n):
                pool.wait_ge(stats_ready, n + 1)
                own.mark(pool.tensor_tensor(dst[:, :], mv[:, :, 1], eps[:, :], ALU.add))
                own.wait()
                pool.tensor_tensor(dst[:, :], dst[:, :], minus_half[:, :], ALU.pow).then_inc(ready, 1)

            def add_bo(n):
                for t in range(TT):
                    i = pool.tensor_tensor(x_bo[:, t, :], x_in[:, t, :], bo_row[:, :], ALU.add)
                i.then_inc(x_bo_ready, 1)

            def k_diag_odd(plan, b, n):
                for m in range(C):
                    wait_read(pool, plan, b, ("k", m))
                    for p in range(HU):
                        dst = k_diag[:, 2 * m + 1, :, QB * p:QB * (p + 1)]
                        keys = k_t[:, m, :].rearrange("r (j k) -> r j k", k=QB)
                        mask = head_mask[:, 2 * p + 1:2 * p + 2]
                        if p == 0:
                            i = pool.tensor_tensor(dst, keys, part(mask, 0, [0, NB], [0, QB]), ALU.mult)
                        else:
                            i = pool.tensor_scalar(dst, keys, mask, 1.0, ALU.mult, ALU.mult)
                    i.then_inc(k_diag_pool, 1)

            def add_bv(b, m):
                pool.wait_ge(ctx_raw_ready, C * b + (m + 1))
                pool.tensor_tensor(attn_t[:, m, :], num[:, m, :], part(bv[:, m:m + 1], 0, [0, S]),
                                   ALU.add).then_inc(attn_ready, 1)

            def iteration(b, prefetch):
                plan = LOOP if prefetch else LAST
                if prefetch:
                    rstd(stats1_ready, rstd1_ready, mv1, rstd1, b + 1)
                add_bv(b, 0)
                add_bv(b, 1)
                if prefetch:
                    k_diag_odd(plan, b, b + 1)
                rstd(stats2_ready, rstd2_ready, mv2, rstd2, b)
                wait_read(pool, plan, b, ("attn_out", TT // 2 - 1))
                for t in range(TT):
                    i = pool.tensor_tensor(x1_b2[:, t, :], x1[:, t, :], b2_row[:, :], ALU.add)
                i.then_inc(x1_b2_ready, 1)
                if prefetch:
                    add_bo(b + 1)

            pool.memset(q_t[:, :, 0:REACH], 0.0)
            pool.memset(q_t[:, :, REACH + S:], 0.0)
            pool.memset(max_diag[:, :, :].bitcast(F32), 0.0)
            pool.memset(minus_half[:, :], -0.5)
            pool.memset(eps[:, :], EPS)
            pool.memset(ones[:, :], 1.0)
            pool.memset(v_ones[:, :, :, :], 0.0).then_inc(zeros_ready, 1)
            pool.wait_ge(zeros_ready, 1)
            rstd(stats1_ready, rstd1_ready, mv1, rstd1, 0)
            k_diag_odd(START, 0, 0)
            pool.wait_ge(const_loaded, 16 * 4)
            add_bo(0)
            PRE = own.n
            with pool.Fori(0, B - 1) as b:
                own.enter(b * 2 + PRE)
                iteration(b, True)
                assert own.n == 2
            own.enter((B - 1) * 2 + PRE)
            iteration(B - 1, False)

        @block.scalar
        def _(act):
            def copy_norm1_t(plan, b, c):
                i = wait_filled(act, plan, b, ("norm1_t", c))
                act.activation(norm1_t[:, c, :], bank[i][:, :], ACT.Identity).then_inc(emptied[i], 1)

            def add_bias(plan, b, kind, dst, bias):
                for m in range(C):
                    i = wait_filled(act, plan, b, (kind, m))
                    act.activation(dst[m], bank[i][:, :], ACT.Identity,
                                   bias=bias[:, m:m + 1]).then_inc(emptied[i], 1)

            q_dst = [q_t[:, m, REACH:REACH + S] for m in range(C)]
            k_dst = [k_t[:, m, :] for m in range(C)]

            def exp_step(plan, b, t):
                if t >= 3:
                    act.wait_ge(probs_used, b * STEPS + (t - 2))
                act.wait_ge(shifted, b * STEPS + (t + 1))
                i, _ = uses_before(plan, b, ("scores", t))
                w = WIN * len(windows_of(t))
                act.activation(probs[:, t % 3, :, :].rearrange("p a b -> p (a b)")[:, 0:w],
                               bank[i][:, 0:w], ACT.Exp, scale=SCALE).then_inc(emptied[i], 1)

            def num_den(plan, b, u):
                m, r = u // 2, 64 * (u % 2)
                i = wait_filled(act, plan, b, ("context", u))
                if u % 2 == 0:
                    if u:
                        act.wait_ge(ctx_raw_ready, C * b + 1)
                act.activation(num[r:r + 64, m, :], bank[i][r:r + 64, :], ACT.Identity)
                act.activation(den[r:r + 64, :], bank[i][64 - r:128 - r, :],
                               ACT.Identity).then_inc(emptied[i], 1)

            def iteration(b, prefetch):
                plan = LOOP if prefetch else LAST
                for t in range(STEPS + 2):
                    if t < STEPS:
                        exp_step(plan, b, t)
                    for u in range(UNITS):
                        if t == last_step(u) + 2:
                            num_den(plan, b, u)
                    if prefetch and t + AHEAD in T1_AT:
                        copy_norm1_t(plan, b, T1_AT.index(t + AHEAD))
                if prefetch:
                    add_bias(plan, b, "q", q_dst, bq)
                    add_bias(plan, b, "k", k_dst, bk)
                for c in range(C):
                    i = wait_filled(act, plan, b, ("norm2_t", c))
                    act.activation(n2_hi[:, c, :], bank[i][:, :], ACT.Identity).then_inc(n2_hi_ready, 1)
                for i in range(FC):
                    k = wait_filled(act, plan, b, ("hidden", i))
                    if i >= 3:
                        act.wait_ge(hid_used, b * FC + (i - 2))
                        act.wait_ge(hid_lo_ready, b * FC + (i - 2))
                    act.activation(hid[:, i % 3, :], bank[k][:, :], ACT.Gelu, bias=b1[:, i:i + 1],
                                   scale=alpha1[:, i:i + 1]).then_inc(emptied[k], 1)
                    wait_read(act, plan, b, ("hidden", i))
                    act.activation(hid_hi[:, i % 3, :], hid[:, i % 3, :],
                                   ACT.Identity).then_inc(hid_hi_ready, 1)
                act.wait_ge(y_ready, b + 1)
                act.dma_start(tokens(out, b * (S * D)), y[:, :, :]).then_inc(y_free, 16)

            act.sem_inc(y_free, 16)
            for c in range(C):
                copy_norm1_t(START, 0, c)
            act.wait_ge(const_loaded, 16 * 4)
            act.wait_ge(zeros_ready, 1)
            add_bias(START, 0, "q", q_dst, bq)
            add_bias(START, 0, "k", k_dst, bk)
            act.wait_ge(w12_loaded, 32)
            act.wait_ge(signs_ready, 4)
            act.activation(w1[:, :, :], w1[:, :, :], ACT.Abs).then_inc(abs_ready, 1)
            act.activation(w2[:, :, :], w2[:, :, :], ACT.Abs).then_inc(abs_ready, 1)
            wait_read(act, START, 0, "alpha1")
            with act.Fori(0, B - 1) as b:
                iteration(b, True)
            iteration(B - 1, False)
            act.wait_ge(y_free, 16 * B + 16)

        @block.vector
        def _(dve):
            own = Own(dve, dve_done)

            def norm(src, stats, mv, stats_ready):
                for t in range(TT):
                    own.mark(dve.bn_stats(stats[:, t, :], src[:, t, :]))
                own.wait()
                dve.memset(wait_slot[:, :], 0.0)
                for t in range(TT):
                    i = dve.bn_aggr(mv[:, t, :], stats[:, t, :])
                i.then_inc(stats_ready, 1)

            def normalize(src, mv, rstd, dst, rstd_ready, ready, n):
                dve.wait_ge(rstd_ready, n + 1)
                for t in range(TT):
                    i = dve.tensor_scalar(dst[:, t, :], src[:, t, :], mv[:, t, 0:1], rstd[:, t:t + 1],
                                          ALU.subtract, ALU.mult)
                i.then_inc(ready, 1)

            def k_diag_even(plan, b):
                for m in range(C):
                    wait_read(dve, plan, b, ("k", m))
                    for p in range(HU):
                        i = dve.tensor_scalar(
                            k_diag[:, 2 * m, :, QB * p:QB * (p + 1)],
                            k_t[:, m, :].rearrange("r (j k) -> r j k", k=QB),
                            head_mask[:, 2 * p:2 * p + 1], None, ALU.mult)
                    i.then_inc(k_diag_dve, 1)

            def v_transpose(plan, b, m):
                i = wait_filled(dve, plan, b, ("v", m))
                dve.transpose(v_t[:, m, :], bank[i][:, :]).then_inc(emptied[i], 1)

            def v_place(plan, b, m):
                wait_read(dve, plan, b, ("v", m))
                for p in range(HU):
                    r = slice(QB * p, QB * (p + 1))
                    dst = v_ones[r, 2 * m, 0, DH * p:DH * (p + 1)]
                    i = dve.tensor_copy(
                        part(dst, 0, [NB * P + 64, 2], [P, NB], [1, DH]),
                        v_t[r, m, :].rearrange("k (j s d) -> k s j d", j=NB, s=2))
                i.then_inc(v_ready, 1)

            def step_max(plan, b, t):
                i = wait_filled(dve, plan, b, ("scores", t))
                for u, j, n, slot in runs_of(t):
                    own.mark(dve.tensor_reduce(
                        part_max[:, u % 2, j + TPAD:j + TPAD + n, :].rearrange("p a b -> p (a b)"),
                        bank[i][:, WIN * slot:WIN * (slot + n)].rearrange("p (a b) -> p a b", b=QB),
                        AX.X, ALU.max, apply_transpose=True))
                own.wait()
                last = None
                for u, i0, i1 in finished_blocks(t):
                    first = part_max[:, u % 2, i0, WB - 1:WB]
                    last = own.mark(dve.tensor_reduce(
                        neg_max[:, u % 2, i0:i1],
                        part(first, 0, [WB, i1 - i0], [WB - 1, WB]),
                        AX.X, ALU.max, negate=True))
                own.wait()
                for u, i0, i1 in finished_blocks(t):
                    n = i1 - i0
                    last = dve.tensor_tensor(
                        max_diag[:, u % 2, REACH + QB * i0:REACH + QB * i1].rearrange("p (a b) -> p a b", b=QB),
                        part(delta, 0, [0, n], [1, QB]),
                        part(neg_max[:, u % 2, i0:i1], 0, [1, n], [0, QB]), ALU.mult)
                last.then_inc(max_ready, 1)

            def reciprocal(piece):
                w = S // 4
                own.mark(dve.reciprocal(den[:, w * piece:w * (piece + 1)],
                                        den[:, w * piece:w * (piece + 1)]))

            def divide(m):
                own.wait()
                dve.tensor_tensor(num[:, m, :], num[:, m, :], den[:, :],
                                  ALU.mult).then_inc(ctx_raw_ready, 1)

            def iteration(b, prefetch):
                plan = LOOP if prefetch else LAST
                recip_at = last_step(1) + AHEAD + 4
                for t in range(STEPS):
                    step_max(plan, b, t)
                    if prefetch and t == 1:
                        dve.wait_ge(x_loaded, 16 * b + 32)
                        norm(x_in, stats1, mv1, stats1_ready)
                    if prefetch and t == 4:
                        normalize(x_in, mv1, rstd1, norm1, rstd1_ready, norm1_ready, b + 1)
                    if recip_at <= t < recip_at + 4:
                        if t == recip_at:
                            wait_read(dve, plan, b, ("context", 0))
                            wait_read(dve, plan, b, ("context", 1))
                        reciprocal(t - recip_at)
                    if t == recip_at + 4:
                        divide(0)
                wait_read(dve, plan, b, ("context", 2))
                wait_read(dve, plan, b, ("context", 3))
                for piece in range(4):
                    reciprocal(piece)
                divide(1)
                if prefetch:
                    k_diag_even(plan, b)
                dve.wait_ge(x_bo_ready, b + 1)
                for i in range(TT):
                    k = wait_filled(dve, plan, b, ("attn_out", i // 2))
                    ins = dve.tensor_tensor(x1[:, i, :], bank[k][:, D * (i % 2):D * (i % 2 + 1)],
                                            x_bo[:, i, :], ALU.add)
                    if i % 2:
                        ins.then_inc(emptied[k], 1)
                for i in range(TT // 2):
                    wait_read(dve, plan, b, ("attn_out", i))
                norm(x1, stats2, mv2, stats2_ready)
                if prefetch:
                    v_transpose(plan, b, 0)
                normalize(x1, mv2, rstd2, norm2, rstd2_ready, norm2_ready, b)
                if prefetch:
                    v_transpose(plan, b, 1)
                    v_place(plan, b, 0)
                for c in range(C):
                    i, _ = uses_before(plan, b, ("norm2_t", c))
                    dve.wait_ge(n2_hi_ready, C * b + (c + 1))
                    dve.tensor_tensor(n2_lo[:, c, :], bank[i][:, :], n2_hi[:, c, :].bitcast(F32),
                                      ALU.subtract).then_inc(emptied[i], 1)
                for i in range(FC):
                    dve.wait_ge(hid_hi_ready, b * FC + (i + 1))
                    dve.tensor_tensor(hid_lo[:, i % 3, :], hid[:, i % 3, :], hid_hi[:, i % 3, :].bitcast(F32),
                                      ALU.subtract).then_inc(hid_lo_ready, 1)
                    if prefetch and i == 0:
                        v_place(plan, b, 1)
                dve.wait_ge(x1_b2_ready, b + 1)
                for i in range(TT):
                    k = wait_filled(dve, plan, b, ("ffn_out", i // 2))
                    ins = dve.tensor_tensor(norm2[:, i, :], bank[k][:, D * (i % 2):D * (i % 2 + 1)],
                                            alpha2[:, :], ALU.mult)
                    if i % 2:
                        ins.then_inc(emptied[k], 1)
                for i in range(TT // 2):
                    wait_read(dve, plan, b, ("ffn_out", i))
                dve.wait_ge(y_free, 16 * b + 16)
                dve.tensor_tensor(y[:, :, :], norm2[:, :, :], x1_b2[:, :, :], ALU.add).then_inc(y_ready, 1)

            dve.memset(part_max[:, :, :, :], -BIG)
            dve.wait_ge(x_loaded, 16)
            norm(x_in, stats1, mv1, stats1_ready)
            normalize(x_in, mv1, rstd1, norm1, rstd1_ready, norm1_ready, 0)
            dve.wait_ge(const_loaded, 16 * 4)
            dve.tensor_copy(quad_ones[:, :], const[:, C_QUAD:C_QUAD + P])
            dve.tensor_copy(ident16[:, :], ident)
            dve.tensor_copy(edge16[:, :, :].rearrange("p a b -> p (a b)"),
                            const[:, C_EDGE:C_END]).then_inc(tables_ready, 1)
            k_diag_even(START, 0)
            dve.wait_ge(zeros_ready, 1)
            for u in range(UNITS):
                dve.tensor_copy(part(v_ones[:, u, 0, 64 * (1 - u % 2):], 0, [P, NB], [DH, HU], [1, DH]),
                                part(const[:, C_QUAD:], 0, [0, NB], [QB, HU], [0, DH]))
            v_transpose(START, 0, 0)
            v_place(START, 0, 0)
            v_transpose(START, 0, 1)
            v_place(START, 0, 1)
            dve.wait_ge(w12_loaded, 32)
            neg = x1[:, :, :].rearrange("p t d -> p (t d)")
            for first, sign in ((0, sign1), (C * F, sign2)):
                flat = sign[:, :, :].rearrange("p a b -> p (a b)")
                for half in range(2):
                    if first or half:
                        dve.wait_ge(signs_ready, 2 * (first > 0) + half)
                    w = raw[:, first + half * TT * D:first + (half + 1) * TT * D]
                    own.mark(dve.tensor_scalar(neg, w, 0.0, None, ALU.is_lt))
                    own.wait()
                    dve.scalar_tensor_tensor(out=flat[:, half * TT * D:(half + 1) * TT * D], in0=w, scalar=0.0,
                                             in1=neg, op0=ALU.is_gt,
                                             op1=ALU.subtract).then_inc(signs_ready, 1)
            i = wait_filled(dve, START, 0, "alpha1")
            dve.tensor_scalar(alpha1[:, :], bank[i][:, 0:FC], 1.0 / D, None, ALU.mult).then_inc(emptied[i], 1)
            i = wait_filled(dve, START, 0, "alpha2")
            dve.tensor_scalar(alpha2[:, :], bank[i][:, 0:D], 1.0 / F, None, ALU.mult).then_inc(emptied[i], 1)
            wait_read(dve, START, 0, "alpha2")
            PRE = own.n
            with dve.Fori(0, B - 1) as b:
                own.enter(b * DVE_OWN + PRE)
                iteration(b, True)
                assert own.n == DVE_OWN, own.n
            own.enter((B - 1) * DVE_OWN + PRE)
            iteration(B - 1, False)

        @block.tensor
        def _(pe):
            def take(plan, b, name):
                i, before = uses_before(plan, b, name)
                if not (isinstance(before, int) and before == 0):
                    pe.wait_ge(emptied[i], before)
                return i

            def transpose_norm(plan, b, kind, src, c):
                i = take(plan, b, (kind, c))
                for t in range(TT):
                    ins = pe.transpose(bank[i][:, P * t:P * (t + 1)], src[:, t, P * c:P * (c + 1)], ident)
                ins.then_inc(filled[i], 1)

            def project(plan, b, kind, w, src):
                for m in range(C):
                    i = take(plan, b, (kind, m))
                    for c in range(C):
                        ins = pe.matmul(bank[i][:, :], w[:, c, P * m:P * (m + 1)], src[:, c, :],
                                        start=(c == 0), stop=(c == C - 1))
                    ins.then_inc(filled[i], 1)

            def scores(plan, b, t):
                i = take(plan, b, ("scores", t))
                n = len(windows_of(t))
                pe.matmul(part(bank[i][:, 0:1], 0, [WIN, n], [WIN - QB, 2], [1, QB]), ident16[:, :],
                          part(edge16[:, 0, 0:1], 0, [0, n], [QB, 2], [1, QB]),
                          start=True, stop=False, skip_group_check=True)
                for u, j, slot in windows_of(t):
                    w0 = 1 if j < TPAD else 0
                    w1_ = WB - 1 if j >= NB - TPAD else WB
                    ins = pe.matmul(bank[i][:, WIN * slot + QB * w0:WIN * slot + QB * w1_],
                                    k_diag[:, u, j, :], q_t[:, u // 2, QB * (j + w0):QB * (j + w1_)],
                                    start=False, stop=False, skip_group_check=True)
                ins.then_inc(filled[i], 1)

            def shift(plan, b, t):
                i, _ = uses_before(plan, b, ("scores", t))
                u, j, _ = windows_of(t)[-1]
                last = NB * u + min(j + 2 * TPAD, NB - 1)
                pe.wait_ge(max_ready, b * STEPS + (last // PER_BANK + 1))
                for u, j, n, slot in runs_of(t):
                    ins = pe.matmul(bank[i][:, WIN * slot:WIN * (slot + n)], quad_ones[:, :],
                                    part(max_diag[:, u % 2, QB * j:QB * j + 1], 0, [QB, n], [1, WIN]),
                                    start=False, stop=True, skip_group_check=True)
                ins.then_inc(shifted, 1)

            def context(plan, b, t):
                wait_read(pe, plan, b, ("scores", t))
                for u, j, slot in windows_of(t):
                    if j == 0:
                        take(plan, b, ("context", u))
                        pe.wait_ge(v_ready, C * b + (u // 2 + 1))
                    i, _ = uses_before(plan, b, ("context", u))
                    i0, i1 = max(0, j - TPAD), min(NB, j + TPAD + 1)
                    w0 = i0 - j + TPAD
                    ins = pe.matmul(bank[i][:, QB * i0:QB * i1], v_ones[:, u, j, :],
                                    probs[:, t % 3, slot, QB * w0:QB * (w0 + i1 - i0)],
                                    start=(j == 0), stop=(j == NB - 1), skip_group_check=True)
                    if j == NB - 1:
                        ins.then_inc(filled[i], 1)
                        ins = None
                if ins is not None:
                    ins.then_inc(probs_used, 1)
                else:
                    pe.sem_inc(probs_used, 1)

            def attention_out(plan, b):
                for i in range(TT):
                    if i % 2 == 0:
                        k = take(plan, b, ("attn_out", i // 2))
                    for m in range(C):
                        ins = pe.matmul(bank[k][:, D * (i % 2):D * (i % 2 + 1)],
                                        attn_t[:, m, P * i:P * (i + 1)], wo[:, m, :],
                                        start=(m == 0 and i % 2 == 0), stop=(m == C - 1),
                                        skip_group_check=True)
                    if i % 2:
                        ins.then_inc(filled[k], 1)

            def hidden(plan, b, i):
                k = take(plan, b, ("hidden", i))
                for c in range(C):
                    for half in (n2_hi, n2_lo):
                        ins = pe.matmul(bank[k][:, :], sign1[:, c, P * i:P * (i + 1)], half[:, c, :],
                                        start=(c == 0 and half is n2_hi),
                                        stop=(c == C - 1 and half is n2_lo))
                ins.then_inc(filled[k], 1)

            def ffn_out(plan, b, i):
                pe.wait_ge(hid_hi_ready, b * FC + (i + 1))
                pe.wait_ge(hid_lo_ready, b * FC + (i + 1))
                for t in range(TT):
                    k, _ = uses_before(plan, b, ("ffn_out", t // 2))
                    if i == 0 and t % 2 == 0:
                        take(plan, b, ("ffn_out", t // 2))
                    for half in (hid_hi, hid_lo):
                        ins = pe.matmul(bank[k][:, D * (t % 2):D * (t % 2 + 1)],
                                        half[:, i % 3, P * t:P * (t + 1)], sign2[:, i, :],
                                        start=(i == 0 and t % 2 == 0 and half is hid_hi),
                                        stop=(i == FC - 1 and half is hid_lo), skip_group_check=True)
                    if i == FC - 1 and t % 2:
                        ins.then_inc(filled[k], 1)
                pe.sem_inc(hid_used, 1) if i == FC - 1 else ins.then_inc(hid_used, 1)

            def iteration(b, prefetch):
                plan = LOOP if prefetch else LAST
                for m in range(C):
                    pe.wait_ge(k_diag_dve, C * b + (m + 1))
                    pe.wait_ge(k_diag_pool, C * b + (m + 1))
                for t in range(STEPS + AHEAD + 1):
                    if t < STEPS:
                        scores(plan, b, t)
                    if t > AHEAD:
                        context(plan, b, t - AHEAD - 1)
                    if AHEAD <= t < STEPS + AHEAD:
                        shift(plan, b, t - AHEAD)
                    if prefetch and t in T1_AT:
                        if t == T1_AT[0]:
                            pe.wait_ge(norm1_ready, b + 2)
                        transpose_norm(plan, b, "norm1_t", norm1, T1_AT.index(t))
                if prefetch:
                    for c in range(C):
                        wait_read(pe, plan, b, ("norm1_t", c))
                    project(plan, b, "q", wq, norm1_t)
                    pe.wait_ge(ctx_loaded, 16 * b + 32)
                    project(plan, b, "k", wk, ctx_in)
                pe.wait_ge(attn_ready, C * b + C)
                attention_out(plan, b)
                if prefetch:
                    project(plan, b, "v", wv, ctx_in)
                pe.wait_ge(norm2_ready, b + 1)
                for c in range(C):
                    transpose_norm(plan, b, "norm2_t", norm2, c)
                for c in range(C):
                    wait_read(pe, plan, b, ("norm2_t", c))
                for i in range(FC + 2):
                    if i < FC:
                        hidden(plan, b, i)
                    if i >= 2:
                        ffn_out(plan, b, i - 2)

            pe.wait_ge(const_loaded, 16 * 4)
            pe.wait_ge(norm1_ready, 1)
            for c in range(C):
                transpose_norm(START, 0, "norm1_t", norm1, c)
            for c in range(C):
                wait_read(pe, START, 0, ("norm1_t", c))
            pe.wait_ge(wq_loaded, 16)
            project(START, 0, "q", wq, norm1_t)
            pe.wait_ge(ctx_loaded, 16)
            pe.wait_ge(wk_loaded, 16)
            project(START, 0, "k", wk, ctx_in)
            pe.wait_ge(wv_loaded, 16)
            project(START, 0, "v", wv, ctx_in)
            pe.wait_ge(zeros_ready, 1)
            pe.wait_ge(abs_ready, 1)
            for i in range(FC):
                for c in range(C):
                    ins = pe.matmul(bank[6][:, i:i + 1], w1[:, c, P * i:P * (i + 1)], ones[:, 0:1],
                                    start=(c == 0), stop=(c == C - 1))
            ins.then_inc(filled[6], 1)
            pe.wait_ge(abs_ready, 2)
            for i in range(FC):
                ins = pe.matmul(bank[7][:, 0:D], ones[:, :], w2[:, i, :], start=(i == 0), stop=(i == FC - 1))
            ins.then_inc(filled[7], 1)
            pe.wait_ge(wo_loaded, 16)
            pe.wait_ge(tables_ready, 1)
            with pe.Fori(0, B - 1) as b:
                iteration(b, True)
            iteration(B - 1, False)


def kernel(x, ctx_1024, L0_xattn_Wq, L0_xattn_bq, L0_xattn_Wk, L0_xattn_bk, L0_xattn_Wv, L0_xattn_bv,
           L0_xattn_Wo, L0_xattn_bo, L0_ffn_w1, L0_ffn_b1, L0_ffn_w2, L0_ffn_b2):
    import numpy as np
    import concourse.bacc as bacc
    from concourse.bass_utils import run_bass_kernel_spmd

    def t(a):
        return np.ascontiguousarray(np.asarray(a).T)

    def by_unit(a):
        a = np.asarray(a)
        shape = a.shape
        return np.ascontiguousarray(a.reshape(C, HU, 2, DH, -1).transpose(0, 2, 1, 3, 4).reshape(shape))

    def columns(a):
        return np.asarray(a).reshape(-1, P).T

    r = np.arange(P)
    k, q = r[:, None] % QB, np.arange(QB)[None, :]
    consts = np.concatenate([
        np.eye(P), r[:, None] // QB == r[None, :] // QB, r[:, None] // DH == np.arange(2 * HU)[None, :],
        k == q, np.where(k > q, -BIG, 0.0), np.where(q > k, -BIG, 0.0)], axis=1).astype(np.float32)

    arrays = {
        "x": np.ascontiguousarray(np.asarray(x)),
        "ctx_t": np.ascontiguousarray(np.asarray(ctx_1024).transpose(0, 2, 1)),
        "wq_t": t(L0_xattn_Wq), "wk_t": t(L0_xattn_Wk), "wv_t": t(L0_xattn_Wv),
        "wo_t": by_unit(t(L0_xattn_Wo)),
        "w1_t": t(L0_ffn_w1), "w2_t": t(L0_ffn_w2),
        "cols": np.ascontiguousarray(np.concatenate(
            [columns(L0_xattn_bq), columns(L0_xattn_bk), columns(by_unit(L0_xattn_bv)),
             columns(L0_ffn_b1)], axis=1)),
        "rows": np.stack([np.asarray(L0_xattn_bo), np.asarray(L0_ffn_b2)]),
        "consts": consts,
    }
    nc = bacc.Bacc("TRN2", target_bir_lowering=False, num_devices=1)
    args = [nc.dram_tensor(name, a.shape, mybir.dt.from_np(a.dtype), kind="ExternalInput").ap()
            for name, a in arrays.items()]
    out = nc.dram_tensor("y_out", (B, S, D), F32, kind="ExternalOutput").ap()
    xattn_ffn_kernel(nc, *args, out)
    r = run_bass_kernel_spmd(nc, [arrays], core_ids=[0])
    return r.results[0]["y_out"]
```

```python
from contextlib import ExitStack

import concourse.bass as bass
from concourse import mybir

ALU = mybir.AluOpType
ACT = mybir.ActivationFunctionType
AX = mybir.AxisListType
F32 = mybir.dt.float32
F32R = mybir.dt.float32r
BF16 = mybir.dt.bfloat16

P = 128
B, S, D = 4, 512, 256
H, DH = 16, 16
F = 1024
REACH = 64
EPS = 1e-5
BIG = 3.0e38

C = D // P
TT = S // P
FC = F // P
QB = 32
NB = S // QB
WB = 2 * REACH // QB + 1
WIN = WB * QB
UNITS = 4
HU = H // UNITS
PER_BANK = 3
NWIN = UNITS * NB
STEPS = -(-NWIN // PER_BANK)
AHEAD = 3
RING = 6
TPAD = REACH // QB
TJ = NB + 2 * TPAD
SCALE = DH ** -0.5

C_IDENT, C_QUAD, C_HEAD, C_DELTA, C_EDGE = 0, 128, 256, 264, 296
C_END = C_EDGE + 2 * QB


def windows_of(t):
    return [(n // NB, n % NB, n - PER_BANK * t)
            for n in range(PER_BANK * t, min(PER_BANK * (t + 1), NWIN))]


def runs_of(t):
    out = []
    for u, j, slot in windows_of(t):
        if out and out[-1][0] == u:
            out[-1][2] += 1
        else:
            out.append([u, j, 1, slot])
    return out


def finished_blocks(t):
    out = []
    for u, j, n, _ in runs_of(t):
        before = max(0, j - TPAD)
        after = NB if j + n == NB else max(0, j + n - TPAD)
        if after > before:
            out.append((u, before, after))
    return out


def last_step(u):
    return (NB * (u + 1) - 1) // PER_BANK


class Banks:

    def __init__(self, names):
        self.place, self.uses = {}, [0] * 8
        for name, i in names:
            self.place[name] = (i, self.uses[i])
            self.uses[i] += 1


T1_AT = (9, 12)
FILL_AT = {STEPS: ("k", 0), STEPS + 1: ("q", 0), STEPS + 2: ("q", 1)}
HALF = S // 2


def bank_uses(prefetch, attention=True, weights=False):
    next_scores = [(("scores of next", t), t) for t in range(AHEAD)]
    if not attention:
        return Banks([(("k", 0), 3), (("k", 1), 4), (("norm1_t", 0), 5), (("norm1_t", 1), 0),
                      (("q", 0), 1), (("q", 1), 2), (("v", 0), 3), (("v", 1), 4)] + next_scores)
    names = []
    for t in range(STEPS + AHEAD + 1):
        if AHEAD <= t < STEPS:
            names.append((("scores", t), t % RING))
        for u in range(UNITS):
            if t - AHEAD - 1 == (NB * u) // PER_BANK:
                names.append((("context", u), 6 + u % 2))
        if prefetch and t in T1_AT:
            names.append((("norm1_t", T1_AT.index(t)), (t + 2) % RING))
        if prefetch and t in FILL_AT:
            names.append((FILL_AT[t], t % RING))
    names += [(("k", 1), 1), (("v", 0), 2)] * prefetch + [("alpha1", 3)] * weights
    names += [(("attn_out", i), (4, 5, 3, 0)[i]) for i in range(TT)]
    names += [(("v", 1), 1)] * prefetch + [("alpha2", 5)] * weights
    names += next_scores * prefetch
    names += [(("norm2_t", 0), 3), (("norm2_t", 1), 4)]
    names += [(("hidden", i), (5, 3, 4)[i % 3]) for i in range(FC)]
    return Banks(names + [(("ffn_out", i), 6 + i) for i in range(2)])


DVE_OWN = 60


def xattn_ffn_kernel(nc, x, ctx_t, wq_t, wk_t, wv_t, wo_t, w1_t, w2_t, cols, rows, consts, out):
    START, FIRST = bank_uses(True, attention=False), bank_uses(True, weights=True)
    LOOP, LAST = bank_uses(True), bank_uses(False)

    with ExitStack() as ctx:
        def sb(name, shape, dt=F32):
            return ctx.enter_context(nc.sbuf_tensor(name, shape, dt))

        def sem(name):
            return ctx.enter_context(nc.semaphore(name))

        bank = [ctx.enter_context(nc.psum_tensor(f"bank{i}", [P, 512], F32)) for i in range(8)]

        wq = sb("wq", [P, C, D])
        wk = sb("wk", [P, C, D])
        wv = sb("wv", [P, C, D])
        wo = sb("wo", [P, C, D])
        raw = sb("raw", [P, 2 * C * F])
        w1 = raw[:, 0:C * F].rearrange("p (c n) -> p c n", c=C)
        w2 = raw[:, C * F:].rearrange("p (c n) -> p c n", c=FC)
        hid = raw[:, 0:3 * S].rearrange("p (i s) -> p i s", i=3)
        x1_b2 = raw[:, 3 * S:5 * S].rearrange("p (t d) -> p t d", t=TT)
        y = raw[:, 5 * S:7 * S].rearrange("p (t d) -> p t d", t=TT)
        sign1 = sb("sign1", [P, C, F], F32R)
        sign2 = sb("sign2", [P, FC, D], F32R)
        alpha1 = sb("alpha1", [P, FC])
        alpha2 = sb("alpha2", [P, D])
        col = sb("col", [P, 3 * C + FC])
        bo_row = sb("bo_row", [P, D])
        b2_row = sb("b2_row", [P, D])
        const = sb("const", [P, C_END])
        quad_ones = sb("quad_ones", [P, P], F32R)
        ident16 = sb("ident16", [P, P], BF16)
        edge16 = sb("edge16", [P, 2, QB], BF16)
        ones = sb("ones", [P, P])
        minus_half = sb("minus_half", [P, TT])
        eps = sb("eps", [P, TT])
        wait_slot = sb("wait_slot", [P, 1])
        ident = const[:, C_IDENT:C_IDENT + P]
        head_mask = const[:, C_HEAD:C_HEAD + 2 * HU]
        delta = const[:, C_DELTA:C_DELTA + QB]
        bq, bk, bv, b1 = col[:, 0:C], col[:, C:2 * C], col[:, 2 * C:3 * C], col[:, 3 * C:]

        x_in = sb("x_in", [P, TT, D])
        ctx_in = sb("ctx_in", [P, C, S])
        x_bo = sb("x_bo", [P, TT, D])
        stats1 = sb("stats1", [P, TT, 6])
        mv1 = sb("mv1", [P, TT, 2])
        rstd1 = sb("rstd1", [P, TT])
        norm1 = sb("norm1", [P, TT, D])
        norm1_t = sb("norm1_t", [P, C, S])
        q_t = sb("q_t", [P, C, S + 2 * REACH])
        k_t = sb("k_t", [P, C, S])
        v_t = sb("v_t", [P, C, S])
        k_diag = sb("k_diag", [P, UNITS, NB, P])
        v_ones = sb("v_ones", [P, UNITS, NB, P])

        part_max = sb("part_max", [P, 2, TJ, WB])
        neg_max = sb("neg_max", [P, 2, NB])
        max_diag = sb("max_diag", [P, 2, S + 2 * REACH], F32R)
        probs = sb("probs", [P, 3, PER_BANK, WIN])
        num = sb("num", [P, C, S])
        den = sb("den", [P, S])
        attn_t = sb("attn_t", [P, C, S])

        x1 = sb("x1", [P, TT, D])
        stats2 = sb("stats2", [P, TT, 6])
        mv2 = sb("mv2", [P, TT, 2])
        rstd2 = sb("rstd2", [P, TT])
        norm2 = sb("norm2", [P, TT, D])
        n2_hi = sb("n2_hi", [P, C, S], F32R)
        n2_lo = sb("n2_lo", [P, C, S], F32R)
        hid_hi = sb("hid_hi", [P, 3, S], F32R)
        hid_lo = sb("hid_lo", [P, 3, S], F32R)

        const_loaded = sem("const_loaded")
        x_loaded = sem("x_loaded")
        ctx_loaded = sem("ctx_loaded")
        wq_loaded, wk_loaded, wv_loaded = sem("wq_loaded"), sem("wk_loaded"), sem("wv_loaded")
        wo_loaded, w12_loaded = sem("wo_loaded"), sem("w12_loaded")
        rows_loaded = sem("rows_loaded")
        y_free = sem("y_free")
        tables_ready = sem("tables_ready")
        zeros_ready = sem("zeros_ready")
        signs_ready = sem("signs_ready")
        abs_ready = sem("abs_ready")
        filled = [sem(f"filled{i}") for i in range(8)]
        emptied = [sem(f"emptied{i}") for i in range(8)]
        dve_done, pool_done = sem("dve_done"), sem("pool_done")
        stats1_ready, rstd1_ready, norm1_ready = sem("stats1_ready"), sem("rstd1_ready"), sem("norm1_ready")
        k_diag_dve, k_diag_pool, v_ready = sem("k_diag_dve"), sem("k_diag_pool"), sem("v_ready")
        x_bo_ready = sem("x_bo_ready")
        max_ready, shifted = sem("max_ready"), sem("shifted")
        half_read = sem("half_read")
        ctx_raw_ready, attn_ready = sem("ctx_raw_ready"), sem("attn_ready")
        x1_b2_ready = sem("x1_b2_ready")
        stats2_ready, rstd2_ready, norm2_ready = sem("stats2_ready"), sem("rstd2_ready"), sem("norm2_ready")
        n2_hi_ready = sem("n2_hi_ready")
        hid_hi_ready, hid_lo_ready = sem("hid_hi_ready"), sem("hid_lo_ready")
        y_ready = sem("y_ready")

        def part(tile_ap, offset, *dims):
            return bass.AP(tile_ap.tensor, tile_ap.offset + offset, [tile_ap.ap[0], *dims])

        def uses_before(plan, b, name):
            if name[0] == "scores" and name[1] < AHEAD:
                name = ("scores of next", name[1])
                if plan is FIRST:
                    plan = START
                else:
                    plan, b, name = of_last_row(plan, b, name)
            i, n = plan.place[name]
            if plan is START:
                return i, n
            if plan is FIRST:
                return i, START.uses[i] + n
            return i, (b - 1) * LOOP.uses[i] + (START.uses[i] + FIRST.uses[i] + n)

        def of_last_row(plan, b, name):
            i, _ = LOOP.place[name]
            assert FIRST.place[name] == LOOP.place[name] and FIRST.uses[i] == LOOP.uses[i]
            return LOOP, b - 1, name

        def wait_filled(eng, plan, b, name):
            i, before = uses_before(plan, b, name)
            eng.wait_ge(filled[i], before + 1)
            return i

        def wait_read(eng, plan, b, name):
            i, before = uses_before(plan, b, name)
            eng.wait_ge(emptied[i], before + 1)

        class Own:

            def __init__(self, eng, done):
                self.eng, self.done, self.base, self.n = eng, done, 0, 0

            def mark(self, ins):
                self.n += 1
                return ins.then_inc(self.done, 1)

            def wait(self):
                self.eng.wait_ge(self.done, self.base + self.n)

            def enter(self, base):
                self.base, self.n = base, 0

        def tokens(dram, offset):
            return bass.AP(dram.tensor, offset, [[D, P], [P * D, TT], [1, D]])

        def features(dram, offset):
            return bass.AP(dram.tensor, offset, [[S, P], [P * S, C], [1, S]])

        block = ctx.enter_context(nc.Block())

        @block.sync
        def _(sp):
            def load_weights(tile, dram, loaded):
                sp.dma_start(tile, dram.rearrange("(c p) n -> p c n", p=P)).then_inc(loaded, 16)

            sp.dma_start(x_in[:, :, :], tokens(x, 0)).then_inc(x_loaded, 16)
            load_weights(wk[:, :, :], wk_t, wk_loaded)
            sp.dma_start(ctx_in[:, :, :], features(ctx_t, 0)).then_inc(ctx_loaded, 16)
            sp.dma_start(const[:, :], consts).then_inc(const_loaded, 16)
            sp.dma_start(col[:, :], cols).then_inc(const_loaded, 16)
            load_weights(wq[:, :, :], wq_t, wq_loaded)
            load_weights(wv[:, :, :], wv_t, wv_loaded)
            sp.dma_start(bo_row[:, :], rows[0:1, :].partition_broadcast(P)).then_inc(rows_loaded, 16)
            sp.dma_start(b2_row[:, :], rows[1:2, :].partition_broadcast(P)).then_inc(rows_loaded, 16)
            load_weights(w1, w1_t, w12_loaded)
            load_weights(w2, w2_t, w12_loaded)
            load_weights(wo[:, :, :], wo_t, wo_loaded)

            def load_row(next_row, rows_done, projected):
                sp.wait_ge(x_bo_ready, rows_done)
                sp.wait_ge(norm1_ready, rows_done)
                sp.wait_ge(v_ready, projected)
                sp.dma_start(x_in[:, :, :], tokens(x, next_row)).then_inc(x_loaded, 16)
                sp.dma_start(ctx_in[:, :, :], features(ctx_t, next_row)).then_inc(ctx_loaded, 16)

            load_row(S * D, 1, C)
            with sp.Fori(1, B - 1) as b:
                next_row = sp.snap(b * (S * D) + S * D)
                rows_done, projected = sp.snap(b + 1), sp.snap(C * b + C)
                load_row(next_row, rows_done, projected)

        @block.gpsimd
        def _(pool):
            own = Own(pool, pool_done)

            def rstd(stats_ready, made, ready, mv, dst, tiles):
                pool.wait_ge(stats_ready, made)
                own.mark(pool.tensor_tensor(dst[:, tiles], mv[:, tiles, 1], eps[:, tiles], ALU.add))
                own.wait()
                pool.tensor_tensor(dst[:, tiles], dst[:, tiles], minus_half[:, tiles],
                                   ALU.pow).then_inc(ready, 1)

            def add_row(dst, src, row, ready):
                pool.tensor_tensor(dst, src, part(row[:, :], 0, [0, TT], [1, D]), ALU.add).then_inc(ready, 1)

            def k_diag_odd(plan, b, m):
                wait_read(pool, plan, b, ("k", m))
                for p in range(HU):
                    dst = k_diag[:, 2 * m + 1, :, QB * p:QB * (p + 1)]
                    keys = k_t[:, m, :].rearrange("r (j k) -> r j k", k=QB)
                    mask = head_mask[:, 2 * p + 1:2 * p + 2]
                    if p == 0:
                        i = pool.tensor_tensor(dst, keys, part(mask, 0, [0, NB], [0, QB]), ALU.mult)
                    else:
                        i = pool.tensor_scalar(dst, keys, mask, 1.0, ALU.mult, ALU.mult)
                i.then_inc(k_diag_pool, 1)

            def add_bv(b, m, half):
                pool.wait_ge(ctx_raw_ready, 2 * C * b + (2 * m + half + 1))
                q = slice(HALF * half, HALF * (half + 1))
                pool.tensor_tensor(attn_t[:, m, q], num[:, m, q], part(bv[:, m:m + 1], 0, [0, HALF]),
                                   ALU.add).then_inc(attn_ready, 1)

            def iteration(plan, b):
                prefetch = plan is not LAST
                if prefetch:
                    rstd(stats1_ready, b + 2, rstd1_ready, mv1, rstd1, slice(0, TT))
                for m in range(C):
                    for half in range(2):
                        add_bv(b, m, half)
                for half in range(2):
                    rstd(stats2_ready, 2 * b + (half + 1), rstd2_ready, mv2, rstd2,
                         slice(TT // 2 * half, TT // 2 * (half + 1)))
                if prefetch:
                    k_diag_odd(plan, b, 0)
                wait_read(pool, plan, b, ("attn_out", TT - 1))
                if plan is FIRST:
                    wait_filled(pool, plan, b, "alpha2")
                add_row(x1_b2, x1[:, :, :], b2_row, x1_b2_ready)
                if prefetch:
                    k_diag_odd(plan, b, 1)
                    add_row(x_bo[:, :, :], x_in[:, :, :], bo_row, x_bo_ready)

            pool.memset(minus_half[:, :], -0.5)
            pool.memset(eps[:, :], EPS)
            pool.memset(ones[:, :], 1.0)
            pool.memset(v_ones[:, :, :, :], 0.0).then_inc(zeros_ready, 1)
            pool.wait_ge(zeros_ready, 1)
            rstd(stats1_ready, 1, rstd1_ready, mv1, rstd1, slice(0, TT))
            pool.wait_ge(const_loaded, 32)
            for m in range(C):
                k_diag_odd(START, 0, m)
            pool.wait_ge(rows_loaded, 32)
            add_row(x_bo[:, :, :], x_in[:, :, :], bo_row, x_bo_ready)
            iteration(FIRST, 0)
            before = own.n
            with pool.Fori(1, B - 1) as b:
                own.enter((b - 1) * 3 + before)
                iteration(LOOP, b)
                assert own.n == 3
            own.enter((B - 2) * 3 + before)
            iteration(LAST, B - 1)

        @block.scalar
        def _(act):
            def copy_norm1_t(plan, b, c):
                i = wait_filled(act, plan, b, ("norm1_t", c))
                act.activation(norm1_t[:, c, :], bank[i][:, :], ACT.Identity).then_inc(emptied[i], 1)

            def project_bias(plan, b, kind, m):
                dst, bias = {"q": (q_dst, bq), "k": (k_dst, bk)}[kind]
                i = wait_filled(act, plan, b, (kind, m))
                act.activation(dst[m], bank[i][:, :], ACT.Identity, bias=bias[:, m:m + 1]).then_inc(emptied[i], 1)

            q_dst = [q_t[:, m, REACH:REACH + S] for m in range(C)]
            k_dst = [k_t[:, m, :] for m in range(C)]

            def exp_step(plan, b, t):
                act.wait_ge(shifted, b * STEPS + (t + 1))
                i, _ = uses_before(plan, b, ("scores", t))
                w = WIN * len(windows_of(t))
                act.activation(probs[:, t % 3, :, :].rearrange("p a b -> p (a b)")[:, 0:w],
                               bank[i][:, 0:w], ACT.Exp, scale=SCALE).then_inc(emptied[i], 1)

            def num_den(plan, b, u, half):
                m, r = u // 2, 64 * (u % 2)
                q = slice(HALF * half, HALF * (half + 1))
                i = wait_filled(act, plan, b, ("context", u))
                if u == 2:
                    act.wait_ge(ctx_raw_ready, 2 * C * b + (half + 1))
                act.activation(num[r:r + 64, m, q], bank[i][r:r + 64, q], ACT.Identity)
                act.activation(den[r:r + 64, q], bank[i][64 - r:128 - r, q],
                               ACT.Identity).then_inc(emptied[i] if half else half_read, 1)

            def size_of_weights(n):
                if n == 0:
                    act.wait_ge(signs_ready, 4)
                w = raw[:, C * F // 2 * n:C * F // 2 * (n + 1)]
                act.activation(w, w, ACT.Abs).then_inc(abs_ready, 1)

            def iteration(plan, b):
                prefetch = plan is not LAST
                for t in range(STEPS + 2):
                    if t < STEPS:
                        exp_step(plan, b, t)
                    if prefetch and t + AHEAD in FILL_AT:
                        project_bias(plan, b, *FILL_AT[t + AHEAD])
                    for u in range(UNITS):
                        if t == last_step(u) + 2:
                            num_den(plan, b, u, 0)
                            num_den(plan, b, u, 1)
                    if prefetch and t + AHEAD in T1_AT:
                        copy_norm1_t(plan, b, T1_AT.index(t + AHEAD))
                    if plan is FIRST and 12 <= t < 16:
                        size_of_weights(t - 12)
                    if plan is not FIRST and t == 6:
                        act.wait_ge(y_ready, b)
                        act.dma_start(tokens(out, (b - 1) * (S * D)), y[:, :, :]).then_inc(y_free, 16)
                if prefetch:
                    project_bias(plan, b, "k", 1)
                for c in range(C):
                    i = wait_filled(act, plan, b, ("norm2_t", c))
                    act.activation(n2_hi[:, c, :], bank[i][:, :], ACT.Identity).then_inc(n2_hi_ready, 1)
                if plan is FIRST:
                    wait_read(act, plan, b, "alpha1")
                for i in range(FC):
                    k = wait_filled(act, plan, b, ("hidden", i))
                    act.activation(hid[:, i % 3, :], bank[k][:, :], ACT.Gelu, bias=b1[:, i:i + 1],
                                   scale=alpha1[:, i:i + 1]).then_inc(emptied[k], 1)
                    wait_read(act, plan, b, ("hidden", i))
                    act.activation(hid_hi[:, i % 3, :], hid[:, i % 3, :],
                                   ACT.Identity).then_inc(hid_hi_ready, 1)

            act.wait_ge(const_loaded, 32)
            for m in range(C):
                project_bias(START, 0, "k", m)
            for c in range(C):
                copy_norm1_t(START, 0, c)
            act.wait_ge(tables_ready, 1)
            for m in range(C):
                project_bias(START, 0, "q", m)
            act.sem_inc(y_free, 16)
            iteration(FIRST, 0)
            with act.Fori(1, B - 1) as b:
                iteration(LOOP, b)
            iteration(LAST, B - 1)
            act.wait_ge(y_ready, B)
            act.dma_start(tokens(out, (B - 1) * S * D), y[:, :, :]).then_inc(y_free, 16)
            act.wait_ge(y_free, 16 * B + 16)

        @block.vector
        def _(dve):
            own = Own(dve, dve_done)

            def statistics(src, stats, mv, stats_ready, tiles):
                for t in tiles:
                    own.mark(dve.bn_stats(stats[:, t, :], src[:, t, :]))
                own.wait()
                dve.memset(wait_slot[:, :], 0.0)
                for t in tiles:
                    i = dve.bn_aggr(mv[:, t, :], stats[:, t, :])
                i.then_inc(stats_ready, 1)

            def normalize(src, mv, rstd, dst, rstd_ready, made, ready, tiles):
                dve.wait_ge(rstd_ready, made)
                for t in tiles:
                    i = dve.tensor_scalar(dst[:, t, :], src[:, t, :], mv[:, t, 0:1], rstd[:, t:t + 1],
                                          ALU.subtract, ALU.mult)
                i.then_inc(ready, 1)

            def k_diag_even(plan, b, m, heads):
                wait_read(dve, plan, b, ("k", m))
                for p in heads:
                    i = dve.tensor_scalar(
                        k_diag[:, 2 * m, :, QB * p:QB * (p + 1)],
                        k_t[:, m, :].rearrange("r (j k) -> r j k", k=QB),
                        head_mask[:, 2 * p:2 * p + 1], None, ALU.mult)
                if HU - 1 in heads:
                    i.then_inc(k_diag_dve, 1)

            def v_transpose(plan, b, m):
                i = wait_filled(dve, plan, b, ("v", m))
                dve.transpose(v_t[:, m, :], bank[i][:, :]).then_inc(emptied[i], 1)

            def v_place(plan, b, m, heads):
                wait_read(dve, plan, b, ("v", m))
                for p in heads:
                    r = slice(QB * p, QB * (p + 1))
                    dst = v_ones[r, 2 * m, 0, DH * p:DH * (p + 1)]
                    i = dve.tensor_copy(
                        part(dst, 0, [NB * P + 64, 2], [P, NB], [1, DH]),
                        v_t[r, m, :].rearrange("k (j s d) -> k s j d", j=NB, s=2))
                if HU - 1 in heads:
                    i.then_inc(v_ready, 1)

            def step_max(plan, b, t, rows_on=0):
                i = wait_filled(dve, plan, b, (("scores", "scores of next")[rows_on], t))
                for u, j, n, slot in runs_of(t):
                    own.mark(dve.tensor_reduce(
                        part_max[:, u % 2, j + TPAD:j + TPAD + n, :].rearrange("p a b -> p (a b)"),
                        bank[i][:, WIN * slot:WIN * (slot + n)].rearrange("p (a b) -> p a b", b=QB),
                        AX.X, ALU.max, apply_transpose=True))
                own.wait()
                for u, i0, i1 in finished_blocks(t):
                    first = part_max[:, u % 2, i0, WB - 1:WB]
                    last = own.mark(dve.tensor_reduce(
                        neg_max[:, u % 2, i0:i1],
                        part(first, 0, [WB, i1 - i0], [WB - 1, WB]),
                        AX.X, ALU.max, negate=True))
                own.wait()
                for u, i0, i1 in finished_blocks(t):
                    n = i1 - i0
                    last = dve.tensor_tensor(
                        max_diag[:, u % 2, REACH + QB * i0:REACH + QB * i1].rearrange("p (a b) -> p a b", b=QB),
                        part(delta, 0, [0, n], [1, QB]),
                        part(neg_max[:, u % 2, i0:i1], 0, [1, n], [0, QB]), ALU.mult)
                last.then_inc(max_ready, 1)

            def reciprocal(q):
                own.mark(dve.reciprocal(den[:, q], den[:, q]))

            def divide(m, half):
                own.wait()
                q = slice(HALF * half, HALF * (half + 1))
                dve.tensor_tensor(num[:, m, q], num[:, m, q], den[:, q], ALU.mult).then_inc(ctx_raw_ready, 1)

            def wait_num_den(plan, b, m, half):
                if half:
                    wait_read(dve, plan, b, ("context", 2 * m))
                    wait_read(dve, plan, b, ("context", 2 * m + 1))
                else:
                    dve.wait_ge(half_read, UNITS * b + (2 * m + 2))

            def sign_of_weights(n):
                if n == 0:
                    dve.wait_ge(w12_loaded, 32)
                neg = x1[:, :, :].rearrange("p t d -> p (t d)")
                w = raw[:, TT * D * n:TT * D * (n + 1)]
                sign = (sign1, sign2)[n // 2][:, :, :].rearrange("p a b -> p (a b)")
                if n:
                    dve.wait_ge(signs_ready, n)
                own.mark(dve.tensor_scalar(neg, w, 0.0, None, ALU.is_lt))
                own.wait()
                dve.scalar_tensor_tensor(out=sign[:, TT * D * (n % 2):TT * D * (n % 2 + 1)], in0=w, scalar=0.0,
                                         in1=neg, op0=ALU.is_gt, op1=ALU.subtract).then_inc(signs_ready, 1)

            def mean_size(plan, name, dst, count):
                i = wait_filled(dve, plan, 0, name)
                dve.tensor_scalar(dst[:, :], bank[i][:, 0:dst.shape[1]], 1.0 / count, None,
                                  ALU.mult).then_inc(emptied[i], 1)

            def residual(plan, b, i):
                k = wait_filled(dve, plan, b, ("attn_out", i))
                dve.tensor_tensor(x1[:, i, :], bank[k][:, 0:D], x_bo[:, i, :], ALU.add).then_inc(emptied[k], 1)

            def statistics2(plan, b, half):
                tiles = range(TT // 2 * half, TT // 2 * (half + 1))
                for i in tiles:
                    wait_read(dve, plan, b, ("attn_out", i))
                statistics(x1, stats2, mv2, stats2_ready, tiles)

            def scale_out(plan, b, i):
                k = wait_filled(dve, *of_last_row(plan, b, ("ffn_out", i)))
                dve.tensor_tensor(norm2[:, 2 * i:2 * i + 2, :], bank[k][:, :].rearrange("p (t d) -> p t d", d=D),
                                  part(alpha2[:, :], 0, [0, 2], [1, D]), ALU.mult).then_inc(emptied[k], 1)

            def finish_row(plan, b):
                for i in range(2):
                    wait_read(dve, *of_last_row(plan, b, ("ffn_out", i)))
                dve.wait_ge(x1_b2_ready, b)
                dve.wait_ge(y_free, 16 * b)
                dve.tensor_tensor(y[:, :, :], norm2[:, :, :], x1_b2[:, :, :], ALU.add).then_inc(y_ready, 1)

            def iteration(plan, b):
                prefetch = plan is not LAST
                recip_at = (last_step(1) + AHEAD + 3, last_step(1) + AHEAD + 5)
                if plan is not FIRST:
                    for i in range(2):
                        scale_out(plan, b, i)
                for t in range(AHEAD, STEPS):
                    step_max(plan, b, t)
                    if plan is not FIRST and t == 4:
                        finish_row(plan, b)
                    if prefetch and t == 5:
                        dve.wait_ge(x_loaded, 16 * b + 32)
                        statistics(x_in, stats1, mv1, stats1_ready, range(TT))
                    if prefetch and t == 7:
                        normalize(x_in, mv1, rstd1, norm1, rstd1_ready, b + 2, norm1_ready, range(TT))
                    if plan is FIRST and 8 <= t < 12:
                        sign_of_weights(t - 8)
                    for half in range(2):
                        for piece in range(2):
                            if t == recip_at[half] + piece:
                                if piece == 0:
                                    wait_num_den(plan, b, 0, half)
                                q0 = HALF * half + HALF // 2 * piece
                                reciprocal(slice(q0, q0 + HALF // 2))
                                if piece == 1:
                                    divide(0, half)
                if prefetch:
                    k_diag_even(plan, b, 0, range(HU))
                for half in range(2):
                    wait_num_den(plan, b, 1, half)
                    reciprocal(slice(HALF * half, HALF * (half + 1)))
                    divide(1, half)
                dve.wait_ge(x_bo_ready, b + 1)
                halves = (range(TT // 2), range(TT // 2, TT))
                for i in halves[0]:
                    residual(plan, b, i)
                statistics2(plan, b, 0)
                if plan is FIRST:
                    mean_size(plan, "alpha1", alpha1, D)
                for i in halves[1]:
                    residual(plan, b, i)
                normalize(x1, mv2, rstd2, norm2, rstd2_ready, 2 * b + 1, norm2_ready, halves[0])
                statistics2(plan, b, 1)
                if prefetch:
                    v_transpose(plan, b, 0)
                    v_transpose(plan, b, 1)
                normalize(x1, mv2, rstd2, norm2, rstd2_ready, 2 * b + 2, norm2_ready, halves[1])
                for c in range(C):
                    i, _ = uses_before(plan, b, ("norm2_t", c))
                    dve.wait_ge(n2_hi_ready, C * b + (c + 1))
                    dve.tensor_tensor(n2_lo[:, c, :], bank[i][:, :], n2_hi[:, c, :].bitcast(F32),
                                      ALU.subtract).then_inc(emptied[i], 1)
                if plan is FIRST:
                    mean_size(plan, "alpha2", alpha2, F)
                for i in range(FC):
                    if prefetch:
                        heads = range(0, 2) if i in (3, 6) else range(2, HU)
                        if i < AHEAD:
                            step_max(plan, b, i, 1)
                        elif i < 5:
                            v_place(plan, b, 0, heads)
                        elif i == 5:
                            k_diag_even(plan, b, 1, range(HU))
                        else:
                            v_place(plan, b, 1, heads)
                    dve.wait_ge(hid_hi_ready, b * FC + (i + 1))
                    dve.tensor_tensor(hid_lo[:, i % 3, :], hid[:, i % 3, :], hid_hi[:, i % 3, :].bitcast(F32),
                                      ALU.subtract).then_inc(hid_lo_ready, 1)

            dve.memset(part_max[:, :, :, :], -BIG)
            dve.memset(max_diag[:, :, :].bitcast(F32), 0.0)
            dve.memset(q_t[:, :, 0:REACH], 0.0)
            dve.memset(q_t[:, :, REACH + S:], 0.0)
            dve.wait_ge(x_loaded, 16)
            statistics(x_in, stats1, mv1, stats1_ready, range(TT))
            dve.wait_ge(const_loaded, 32)
            dve.tensor_copy(quad_ones[:, :], const[:, C_QUAD:C_QUAD + P])
            dve.tensor_copy(ident16[:, :], ident)
            dve.tensor_copy(edge16[:, :, :].rearrange("p a b -> p (a b)"),
                            const[:, C_EDGE:C_END]).then_inc(tables_ready, 1)
            normalize(x_in, mv1, rstd1, norm1, rstd1_ready, 1, norm1_ready, range(TT))
            for m in range(C):
                k_diag_even(START, 0, m, range(HU))
            dve.wait_ge(zeros_ready, 1)
            for m in range(C):
                for u in (2 * m, 2 * m + 1):
                    dve.tensor_copy(part(v_ones[:, u, 0, 64 * (1 - u % 2):], 0, [P, NB], [DH, HU], [1, DH]),
                                    part(const[:, C_QUAD:], 0, [0, NB], [QB, HU], [0, DH]))
                v_transpose(START, 0, m)
                v_place(START, 0, m, range(HU))
            for t in range(AHEAD):
                step_max(START, -1, t, 1)
            iteration(FIRST, 0)
            before = own.n
            with dve.Fori(1, B - 1) as b:
                own.enter((b - 1) * DVE_OWN + before)
                iteration(LOOP, b)
                assert own.n == DVE_OWN, own.n
            own.enter((B - 2) * DVE_OWN + before)
            iteration(LAST, B - 1)
            for i in range(2):
                scale_out(LAST, B, i)
            finish_row(LAST, B)

        @block.tensor
        def _(pe):
            def take(plan, b, name):
                i, before = uses_before(plan, b, name)
                if not (isinstance(before, int) and before == 0):
                    pe.wait_ge(emptied[i], before)
                return i

            def transpose_norm(plan, b, kind, src, c, tiles=range(TT)):
                i, _ = uses_before(plan, b, (kind, c))
                if 0 in tiles:
                    take(plan, b, (kind, c))
                for t in tiles:
                    ins = pe.transpose(bank[i][:, P * t:P * (t + 1)], src[:, t, P * c:P * (c + 1)], ident)
                if TT - 1 in tiles:
                    ins.then_inc(filled[i], 1)

            def project(plan, b, kind, m):
                w, src = {"q": (wq, norm1_t), "k": (wk, ctx_in), "v": (wv, ctx_in)}[kind]
                i = take(plan, b, (kind, m))
                for c in range(C):
                    ins = pe.matmul(bank[i][:, :], w[:, c, P * m:P * (m + 1)], src[:, c, :],
                                    start=(c == 0), stop=(c == C - 1))
                ins.then_inc(filled[i], 1)

            def scores(plan, b, t, rows_on=0):
                i = take(plan, b, (("scores", "scores of next")[rows_on], t))
                b = b + rows_on
                n = len(windows_of(t))
                pe.matmul(part(bank[i][:, 0:1], 0, [WIN, n], [WIN - QB, 2], [1, QB]), ident16[:, :],
                          part(edge16[:, 0, 0:1], 0, [0, n], [QB, 2], [1, QB]),
                          start=True, stop=False, skip_group_check=True)
                for u, j, slot in windows_of(t):
                    if j == 0 and u % 2 == 0:
                        pe.wait_ge(k_diag_dve, C * b + (u // 2 + 1))
                    if j == 0 and u % 2 == 1:
                        pe.wait_ge(k_diag_pool, C * b + (u // 2 + 1))
                    w0 = 1 if j < TPAD else 0
                    w1_ = WB - 1 if j >= NB - TPAD else WB
                    ins = pe.matmul(bank[i][:, WIN * slot + QB * w0:WIN * slot + QB * w1_],
                                    k_diag[:, u, j, :], q_t[:, u // 2, QB * (j + w0):QB * (j + w1_)],
                                    start=False, stop=False, skip_group_check=True)
                ins.then_inc(filled[i], 1)

            def shift(plan, b, t):
                i, _ = uses_before(plan, b, ("scores", t))
                u, j, _ = windows_of(t)[-1]
                last = NB * u + min(j + 2 * TPAD, NB - 1)
                pe.wait_ge(max_ready, b * STEPS + (last // PER_BANK + 1))
                for u, j, n, slot in runs_of(t):
                    ins = pe.matmul(bank[i][:, WIN * slot:WIN * (slot + n)], quad_ones[:, :],
                                    part(max_diag[:, u % 2, QB * j:QB * j + 1], 0, [QB, n], [1, WIN]),
                                    start=False, stop=True, skip_group_check=True)
                ins.then_inc(shifted, 1)

            def context(plan, b, t):
                wait_read(pe, plan, b, ("scores", t))
                for u, j, slot in windows_of(t):
                    if j == 0:
                        take(plan, b, ("context", u))
                        pe.wait_ge(v_ready, C * b + (u // 2 + 1))
                    i, _ = uses_before(plan, b, ("context", u))
                    i0, i1 = max(0, j - TPAD), min(NB, j + TPAD + 1)
                    w0 = i0 - j + TPAD
                    ins = pe.matmul(bank[i][:, QB * i0:QB * i1], v_ones[:, u, j, :],
                                    probs[:, t % 3, slot, QB * w0:QB * (w0 + i1 - i0)],
                                    start=(j == 0), stop=(j == NB - 1), skip_group_check=True)
                    if j == NB - 1:
                        ins.then_inc(filled[i], 1)

            def attention_out(plan, b, i):
                pe.wait_ge(attn_ready, 2 * C * b + (2 * C - 1 + i // (TT // 2)))
                k = take(plan, b, ("attn_out", i))
                for m in range(C):
                    ins = pe.matmul(bank[k][:, 0:D], attn_t[:, m, P * i:P * (i + 1)], wo[:, m, :],
                                    start=(m == 0), stop=(m == C - 1))
                ins.then_inc(filled[k], 1)

            def sums_of_sizes(plan, which):
                k = take(plan, 0, which)
                pe.wait_ge(abs_ready, 2 if which == "alpha1" else 4)
                for i in range(FC):
                    if which == "alpha1":
                        for c in range(C):
                            ins = pe.matmul(bank[k][:, i:i + 1], w1[:, c, P * i:P * (i + 1)], ones[:, 0:1],
                                            start=(c == 0), stop=(c == C - 1))
                    else:
                        ins = pe.matmul(bank[k][:, 0:D], ones[:, :], w2[:, i, :],
                                        start=(i == 0), stop=(i == FC - 1))
                ins.then_inc(filled[k], 1)

            def hidden(plan, b, i):
                k = take(plan, b, ("hidden", i))
                for half in (n2_hi, n2_lo):
                    for c in range(C):
                        if i == 0 and half is n2_hi:
                            pe.wait_ge(n2_hi_ready, C * b + (c + 1))
                        if i == 0 and half is n2_lo:
                            wait_read(pe, plan, b, ("norm2_t", c))
                        ins = pe.matmul(bank[k][:, :], sign1[:, c, P * i:P * (i + 1)], half[:, c, :],
                                        start=(c == 0 and half is n2_hi),
                                        stop=(c == C - 1 and half is n2_lo))
                ins.then_inc(filled[k], 1)

            def ffn_out(plan, b, i):
                for half in (hid_hi, hid_lo):
                    pe.wait_ge(hid_hi_ready if half is hid_hi else hid_lo_ready, b * FC + (i + 1))
                    for t in range(TT):
                        k, _ = uses_before(plan, b, ("ffn_out", t // 2))
                        if i == 0 and t % 2 == 0 and half is hid_hi:
                            take(plan, b, ("ffn_out", t // 2))
                        ins = pe.matmul(bank[k][:, D * (t % 2):D * (t % 2 + 1)],
                                        half[:, i % 3, P * t:P * (t + 1)], sign2[:, i, :],
                                        start=(i == 0 and t % 2 == 0 and half is hid_hi),
                                        stop=(i == FC - 1 and half is hid_lo), skip_group_check=True)
                        if i == FC - 1 and t % 2 and half is hid_lo:
                            ins.then_inc(filled[k], 1)

            def iteration(plan, b):
                prefetch = plan is not LAST
                for t in range(AHEAD, STEPS + AHEAD + 1):
                    if AHEAD <= t < STEPS:
                        scores(plan, b, t)
                    if t > AHEAD:
                        context(plan, b, t - AHEAD - 1)
                    if AHEAD <= t < STEPS + AHEAD:
                        shift(plan, b, t - AHEAD)
                    if prefetch and t in T1_AT:
                        if t == T1_AT[0]:
                            pe.wait_ge(norm1_ready, b + 2)
                        transpose_norm(plan, b, "norm1_t", norm1, T1_AT.index(t))
                    if prefetch and t in FILL_AT:
                        if t == STEPS:
                            for c in range(C):
                                wait_read(pe, plan, b, ("norm1_t", c))
                            pe.wait_ge(ctx_loaded, 16 * b + 32)
                        project(plan, b, *FILL_AT[t])
                if plan is FIRST:
                    pe.wait_ge(wo_loaded, 16)
                if prefetch:
                    project(plan, b, "k", 1)
                    project(plan, b, "v", 0)
                if plan is FIRST:
                    sums_of_sizes(plan, "alpha1")
                for i in range(TT):
                    attention_out(plan, b, i)
                if prefetch:
                    project(plan, b, "v", 1)
                if plan is FIRST:
                    sums_of_sizes(plan, "alpha2")
                if prefetch:
                    scores(plan, b, 0, 1)
                for half in range(2):
                    if half and prefetch:
                        for t in range(1, AHEAD):
                            scores(plan, b, t, 1)
                    pe.wait_ge(norm2_ready, 2 * b + (half + 1))
                    for c in range(C):
                        transpose_norm(plan, b, "norm2_t", norm2, c,
                                       range(TT // 2 * half, TT // 2 * (half + 1)))
                for i in range(FC + 2):
                    if i < FC:
                        hidden(plan, b, i)
                    if i >= 2:
                        ffn_out(plan, b, i - 2)

            pe.wait_ge(ctx_loaded, 16)
            pe.wait_ge(wk_loaded, 16)
            for m in range(C):
                project(START, 0, "k", m)
            pe.wait_ge(const_loaded, 32)
            pe.wait_ge(norm1_ready, 1)
            for c in range(C):
                transpose_norm(START, 0, "norm1_t", norm1, c)
            for c in range(C):
                wait_read(pe, START, 0, ("norm1_t", c))
            pe.wait_ge(wq_loaded, 16)
            for m in range(C):
                project(START, 0, "q", m)
            pe.wait_ge(wv_loaded, 16)
            for m in range(C):
                project(START, 0, "v", m)
            for m in range(C):
                wait_read(pe, START, 0, ("q", m))
            pe.wait_ge(tables_ready, 1)
            pe.wait_ge(zeros_ready, 1)
            for t in range(AHEAD):
                scores(START, -1, t, 1)
            iteration(FIRST, 0)
            with pe.Fori(1, B - 1) as b:
                iteration(LOOP, b)
            iteration(LAST, B - 1)


def kernel(x, ctx_1024, L0_xattn_Wq, L0_xattn_bq, L0_xattn_Wk, L0_xattn_bk, L0_xattn_Wv, L0_xattn_bv,
           L0_xattn_Wo, L0_xattn_bo, L0_ffn_w1, L0_ffn_b1, L0_ffn_w2, L0_ffn_b2):
    import numpy as np
    import concourse.bacc as bacc
    from concourse.bass_utils import run_bass_kernel_spmd

    def t(a):
        return np.ascontiguousarray(np.asarray(a).T)

    def by_unit(a):
        a = np.asarray(a)
        shape = a.shape
        return np.ascontiguousarray(a.reshape(C, HU, 2, DH, -1).transpose(0, 2, 1, 3, 4).reshape(shape))

    def columns(a):
        return np.asarray(a).reshape(-1, P).T

    r = np.arange(P)
    k, q = r[:, None] % QB, np.arange(QB)[None, :]
    consts = np.concatenate([
        np.eye(P), r[:, None] // QB == r[None, :] // QB, r[:, None] // DH == np.arange(2 * HU)[None, :],
        k == q, np.where(k > q, -BIG, 0.0), np.where(q > k, -BIG, 0.0)], axis=1).astype(np.float32)

    arrays = {
        "x": np.ascontiguousarray(np.asarray(x)),
        "ctx_t": np.ascontiguousarray(np.asarray(ctx_1024).transpose(0, 2, 1)),
        "wq_t": t(L0_xattn_Wq), "wk_t": t(L0_xattn_Wk), "wv_t": t(L0_xattn_Wv),
        "wo_t": by_unit(t(L0_xattn_Wo)),
        "w1_t": t(L0_ffn_w1), "w2_t": t(L0_ffn_w2),
        "cols": np.ascontiguousarray(np.concatenate(
            [columns(L0_xattn_bq), columns(L0_xattn_bk), columns(by_unit(L0_xattn_bv)),
             columns(L0_ffn_b1)], axis=1)),
        "rows": np.stack([np.asarray(L0_xattn_bo), np.asarray(L0_ffn_b2)]),
        "consts": consts,
    }
    nc = bacc.Bacc("TRN2", target_bir_lowering=False, num_devices=1)
    args = [nc.dram_tensor(name, a.shape, mybir.dt.from_np(a.dtype), kind="ExternalInput").ap()
            for name, a in arrays.items()]
    out = nc.dram_tensor("y_out", (B, S, D), F32, kind="ExternalOutput").ap()
    xattn_ffn_kernel(nc, *args, out)
    r = run_bass_kernel_spmd(nc, [arrays], core_ids=[0])
    return r.results[0]["y_out"]
```

```python
from contextlib import ExitStack

import concourse.bass as bass
from concourse import mybir

ALU = mybir.AluOpType
ACT = mybir.ActivationFunctionType
AX = mybir.AxisListType
F32 = mybir.dt.float32
F32R = mybir.dt.float32r
BF16 = mybir.dt.bfloat16

P = 128
B, S, D = 4, 512, 256
H, DH = 16, 16
F = 1024
REACH = 64
EPS = 1e-5
BIG = 3.0e38

C = D // P
TT = S // P
FC = F // P
QB = 32
NB = S // QB
WB = 2 * REACH // QB + 1
WIN = WB * QB
UNITS = 4
HU = H // UNITS
PER_BANK = 3
NWIN = UNITS * NB
STEPS = -(-NWIN // PER_BANK)
AHEAD = 3
RING = 6
TPAD = REACH // QB
TJ = NB + 2 * TPAD
SCALE = DH ** -0.5

C_IDENT, C_QUAD, C_HEAD, C_DELTA, C_EDGE = 0, 128, 256, 264, 296
C_END = C_EDGE + 2 * QB


def windows_of(t):
    return [(n // NB, n % NB, n - PER_BANK * t)
            for n in range(PER_BANK * t, min(PER_BANK * (t + 1), NWIN))]


def runs_of(t):
    out = []
    for u, j, slot in windows_of(t):
        if out and out[-1][0] == u:
            out[-1][2] += 1
        else:
            out.append([u, j, 1, slot])
    return out


def finished_blocks(t):
    out = []
    for u, j, n, _ in runs_of(t):
        before = max(0, j - TPAD)
        after = NB if j + n == NB else max(0, j + n - TPAD)
        if after > before:
            out.append((u, before, after))
    return out


def last_step(u):
    return (NB * (u + 1) - 1) // PER_BANK


class Banks:

    def __init__(self, names):
        self.place, self.uses = {}, [0] * 8
        for name, i in names:
            self.place[name] = (i, self.uses[i])
            self.uses[i] += 1


T1_AT = (12, 15)
HALF = S // 2


def bank_uses(prefetch, attention=True, weights=False):
    next_scores = [(("scores of next", t), t) for t in range(AHEAD)]
    if not attention:
        return Banks([(("k", 0), 3), (("k", 1), 4), (("v", 0), 5), (("v", 1), 0), (("norm1_t", 0), 1),
                      (("norm1_t", 1), 2), (("q", 0), 3), (("q", 1), 4), ("bias_out", 7)] + next_scores)
    names = []
    for t in range(AHEAD, STEPS):
        names.append((("scores", t), t % RING))
        for u in range(UNITS):
            if t - AHEAD - 1 == (NB * u) // PER_BANK:
                names.append((("context", u), 6 + u % 2))
        if prefetch and t in T1_AT:
            names.append((("norm1_t", T1_AT.index(t)), (t + 2) % RING))
    names += [(("k", 0), 4), (("q", 0), 0), (("q", 1), 1), (("k", 1), 5)] * prefetch
    names += [("alpha1", 3)] * weights + [(("v", 0), 2)] * prefetch
    names += [(("attn_out", i), (4, 5, 3, 1)[i]) for i in range(TT)]
    names += [(("v", 1), 2)] * prefetch + [("alpha2", 5)] * weights
    names += next_scores * prefetch
    names += [(("norm2_t", n), (3, 4)[n % C]) for n in range(C)]
    names += [(("norm2_t", C + n), ((3, 4) if prefetch else (0, 1))[n]) for n in range(C)]
    names += [(("hidden", n), (5, 3, 4)[n % 3]) for n in range(FC if prefetch else 2 * FC)]
    return Banks(names + [(("ffn_out", i), 6 + i) for i in range(2)])


def hidden_pieces(last):
    if last:
        return [(n, n % FC, slice(HALF * (n // FC), HALF * (n // FC + 1))) for n in range(2 * FC)]
    return [(n, n, slice(0, S)) for n in range(FC)]


SECOND_AT = 2
DVE_OWN = 60


def xattn_ffn_kernel(nc, x, ctx_t, wq_t, wk_t, wv_t, wo_t, w1_t, w2_t, cols, rows, consts, out):
    START, FIRST = bank_uses(True, attention=False), bank_uses(True, weights=True)
    LOOP, LAST = bank_uses(True), bank_uses(False)

    with ExitStack() as ctx:
        def sb(name, shape, dt=F32):
            return ctx.enter_context(nc.sbuf_tensor(name, shape, dt))

        def sem(name):
            return ctx.enter_context(nc.semaphore(name))

        bank = [ctx.enter_context(nc.psum_tensor(f"bank{i}", [P, 512], F32)) for i in range(8)]

        wq = sb("wq", [P, C, D])
        wk = sb("wk", [P, C, D])
        wv = sb("wv", [P, C, D])
        wo = sb("wo", [P, C, D])
        raw = sb("raw", [P, 2 * C * F])
        w1 = raw[:, 0:C * F].rearrange("p (c n) -> p c n", c=C)
        w2 = raw[:, C * F:].rearrange("p (c n) -> p c n", c=FC)
        hid = raw[:, 0:3 * S].rearrange("p (i s) -> p i s", i=3)
        x1_b2 = raw[:, 3 * S:5 * S].rearrange("p (t d) -> p t d", t=TT)
        y = raw[:, 5 * S:7 * S].rearrange("p (t d) -> p t d", t=TT)
        w_hi = sb("w_hi", [P, 4, C, D], F32R)
        w_lo = sb("w_lo", [P, 4, C, D], F32R)
        sign1 = sb("sign1", [P, C, F], F32R)
        sign2 = sb("sign2", [P, FC, D], F32R)
        alpha1 = sb("alpha1", [P, FC])
        alpha2 = sb("alpha2", [P, D])
        col = sb("col", [P, 3 * C + FC])
        bo_row = sb("bo_row", [P, D])
        b2_row = sb("b2_row", [P, D])
        const = sb("const", [P, C_END])
        quad_ones = sb("quad_ones", [P, P], F32R)
        ident16 = sb("ident16", [P, P], BF16)
        edge16 = sb("edge16", [P, 2, QB], BF16)
        ones = sb("ones", [P, P])
        minus_half = sb("minus_half", [P, TT])
        eps = sb("eps", [P, TT])
        wait_slot = sb("wait_slot", [P, 2])
        ident = const[:, C_IDENT:C_IDENT + P]
        head_mask = const[:, C_HEAD:C_HEAD + 2 * HU]
        delta = const[:, C_DELTA:C_DELTA + QB]
        bq, bk, bv, b1 = col[:, 0:C], col[:, C:2 * C], col[:, 2 * C:3 * C], col[:, 3 * C:]

        x_in = sb("x_in", [P, TT, D])
        ctx_in = sb("ctx_in", [P, C, S])
        x_bo = sb("x_bo", [P, TT, D])
        stats1 = sb("stats1", [P, TT, 6])
        mv1 = sb("mv1", [P, TT, 2])
        rstd1 = sb("rstd1", [P, TT])
        norm1 = sb("norm1", [P, TT, D])
        q_t = sb("q_t", [P, C, S + 2 * REACH])
        k_t = sb("k_t", [P, C, S])
        k_diag = sb("k_diag", [P, UNITS, NB, P])
        v_ones = sb("v_ones", [P, UNITS, NB, P])

        part_max = sb("part_max", [P, 2, TJ, WB])
        neg_max = sb("neg_max", [P, 2, NB])
        max_diag = sb("max_diag", [P, 2, S + 2 * REACH], F32R)
        probs = sb("probs", [P, 3, PER_BANK, WIN])
        num = sb("num", [P, C, S])
        den = sb("den", [P, S])
        v_t = num
        attn_hi = sb("attn_hi", [P, C, S], F32R)
        attn_lo = sb("attn_lo", [P, C, S], F32R)

        x1 = sb("x1", [P, TT, D])
        norm1_t = x1[:, :, :].rearrange("p t d -> p (t d)").rearrange("p (c s) -> p c s", c=C)
        stats2 = sb("stats2", [P, TT, 6])
        mv2 = sb("mv2", [P, TT, 2])
        rstd2 = sb("rstd2", [P, TT])
        norm2 = sb("norm2", [P, TT, D])
        n2_hi = sb("n2_hi", [P, C, S], F32R)
        n2_lo = sb("n2_lo", [P, C, S], F32R)
        hid_hi = sb("hid_hi", [P, 3, S], F32R)
        hid_lo = sb("hid_lo", [P, 3, S], F32R)
        norm1_hi, norm1_lo = n2_hi, n2_lo
        ctx_hi, ctx_lo = hid_hi[:, 0:C, :], hid_lo[:, 0:C, :]

        const_loaded = sem("const_loaded")
        x_loaded = sem("x_loaded")
        ctx_loaded = sem("ctx_loaded")
        wq_loaded, wk_loaded, wv_loaded = sem("wq_loaded"), sem("wk_loaded"), sem("wv_loaded")
        wo_loaded, w12_loaded = sem("wo_loaded"), sem("w12_loaded")
        rows_loaded = sem("rows_loaded")
        y_free = sem("y_free")
        tables_ready = sem("tables_ready")
        ones_ready, zeros_ready = sem("ones_ready"), sem("zeros_ready")
        signs_ready = sem("signs_ready")
        abs_ready, folded = sem("abs_ready"), sem("folded")
        filled = [sem(f"filled{i}") for i in range(8)]
        emptied = [sem(f"emptied{i}") for i in range(8)]
        dve_done, pool_done = sem("dve_done"), sem("pool_done")
        stats1_ready, rstd1_ready, norm1_ready = sem("stats1_ready"), sem("rstd1_ready"), sem("norm1_ready")
        norm1_hi_ready = sem("norm1_hi_ready")
        ctx_hi_ready, ctx_lo_ready = sem("ctx_hi_ready"), sem("ctx_lo_ready")
        w_hi_ready, w_lo_ready = sem("w_hi_ready"), sem("w_lo_ready")
        bv_wo_ready = sem("bv_wo_ready")
        k_diag_dve, k_diag_pool, v_ready = sem("k_diag_dve"), sem("k_diag_pool"), sem("v_ready")
        x_bo_ready = sem("x_bo_ready")
        max_ready, shifted = sem("max_ready"), sem("shifted")
        half_read = sem("half_read")
        ctx_raw_ready, attn_hi_ready, attn_ready = sem("ctx_raw_ready"), sem("attn_hi_ready"), sem("attn_ready")
        x1_b2_ready = sem("x1_b2_ready")
        stats2_ready, rstd2_ready, norm2_ready = sem("stats2_ready"), sem("rstd2_ready"), sem("norm2_ready")
        n2_hi_ready = sem("n2_hi_ready")
        hid_hi_ready, hid_lo_ready = sem("hid_hi_ready"), sem("hid_lo_ready")
        y_ready = sem("y_ready")

        def part(tile_ap, offset, *dims):
            return bass.AP(tile_ap.tensor, tile_ap.offset + offset, [tile_ap.ap[0], *dims])

        def uses_before(plan, b, name):
            if name[0] == "scores" and name[1] < AHEAD:
                name = ("scores of next", name[1])
                if plan is FIRST:
                    plan = START
                else:
                    plan, b, name = of_last_row(plan, b, name)
            i, n = plan.place[name]
            if plan is START:
                return i, n
            if plan is FIRST:
                return i, START.uses[i] + n
            return i, (b - 1) * LOOP.uses[i] + (START.uses[i] + FIRST.uses[i] + n)

        def of_last_row(plan, b, name):
            i, _ = LOOP.place[name]
            assert FIRST.place[name] == LOOP.place[name] and FIRST.uses[i] == LOOP.uses[i]
            return LOOP, b - 1, name

        def wait_filled(eng, plan, b, name):
            i, before = uses_before(plan, b, name)
            eng.wait_ge(filled[i], before + 1)
            return i

        def wait_read(eng, plan, b, name):
            i, before = uses_before(plan, b, name)
            eng.wait_ge(emptied[i], before + 1)

        class Own:

            def __init__(self, eng, done):
                self.eng, self.done, self.base, self.n = eng, done, 0, 0

            def mark(self, ins):
                self.n += 1
                return ins.then_inc(self.done, 1)

            def wait(self):
                self.eng.wait_ge(self.done, self.base + self.n)

            def enter(self, base):
                self.base, self.n = base, 0

        def tokens(dram, offset):
            return bass.AP(dram.tensor, offset, [[D, P], [P * D, TT], [1, D]])

        def features(dram, offset):
            return bass.AP(dram.tensor, offset, [[S, P], [P * S, C], [1, S]])

        block = ctx.enter_context(nc.Block())

        @block.sync
        def _(sp):
            def load_weights(tile, dram, loaded):
                sp.dma_start(tile, dram.rearrange("(c p) n -> p c n", p=P)).then_inc(loaded, 16)

            sp.dma_start(ctx_in[:, :, :], features(ctx_t, 0)).then_inc(ctx_loaded, 16)
            sp.dma_start(x_in[:, :, :], tokens(x, 0)).then_inc(x_loaded, 16)
            load_weights(wv[:, :, :], wv_t, wv_loaded)
            load_weights(wq[:, :, :], wq_t, wq_loaded)
            sp.dma_start(bo_row[:, :], rows[0:1, :].partition_broadcast(P)).then_inc(rows_loaded, 16)
            sp.dma_start(b2_row[:, :], rows[1:2, :].partition_broadcast(P)).then_inc(rows_loaded, 16)
            load_weights(wo[:, :, :], wo_t, wo_loaded)
            load_weights(w1, w1_t, w12_loaded)
            load_weights(w2, w2_t, w12_loaded)

            def load_row(next_row, rows_done, projected):
                sp.wait_ge(x_bo_ready, rows_done)
                sp.wait_ge(norm1_ready, rows_done)
                sp.dma_start(x_in[:, :, :], tokens(x, next_row)).then_inc(x_loaded, 16)
                sp.wait_ge(v_ready, projected)
                sp.dma_start(ctx_in[:, :, :], features(ctx_t, next_row)).then_inc(ctx_loaded, 16)

            load_row(S * D, 1, C)
            with sp.Fori(1, B - 1) as b:
                next_row = sp.snap(b * (S * D) + S * D)
                rows_done, projected = sp.snap(b + 1), sp.snap(C * b + C)
                load_row(next_row, rows_done, projected)
            for i in range(2):
                sp.wait_ge(y_ready, B + i)
                sp.dma_start(tokens(out, (B - 1) * S * D)[:, 2 * i:2 * i + 2, :],
                             y[:, 2 * i:2 * i + 2, :]).then_inc(y_free, 16)
            sp.wait_ge(y_free, 16 * B + 32)

        @block.gpsimd
        def _(pool):
            own = Own(pool, pool_done)

            def rstd(stats_ready, made, ready, mv, dst, tiles):
                pool.wait_ge(stats_ready, made)
                own.mark(pool.tensor_tensor(dst[:, tiles], mv[:, tiles, 1], eps[:, tiles], ALU.add))
                own.wait()
                pool.tensor_tensor(dst[:, tiles], dst[:, tiles], minus_half[:, tiles],
                                   ALU.pow).then_inc(ready, 1)

            def add_row(dst, src, row, ready):
                pool.tensor_tensor(dst, src, part(row[:, :], 0, [0, TT], [1, D]), ALU.add).then_inc(ready, 1)

            def k_diag_odd(plan, b, m):
                wait_read(pool, plan, b, ("k", m))
                for p in range(HU):
                    dst = k_diag[:, 2 * m + 1, :, QB * p:QB * (p + 1)]
                    keys = k_t[:, m, :].rearrange("r (j k) -> r j k", k=QB)
                    mask = head_mask[:, 2 * p + 1:2 * p + 2]
                    if p == 0:
                        i = pool.tensor_tensor(dst, keys, part(mask, 0, [0, NB], [0, QB]), ALU.mult)
                    else:
                        i = pool.tensor_scalar(dst, keys, mask, 1.0, ALU.mult, ALU.mult)
                i.then_inc(k_diag_pool, 1)

            def lower_attn(b, m, half):
                pool.wait_ge(attn_hi_ready, 2 * C * b + (2 * m + half + 1))
                q = slice(HALF * half, HALF * (half + 1))
                pool.tensor_tensor(attn_lo[:, m, q], num[:, m, q], attn_hi[:, m, q].bitcast(F32),
                                  ALU.subtract).then_inc(attn_ready, 1)

            def fold_sizes(w, chunks, sized):
                pool.wait_ge(abs_ready, sized)
                while chunks > 1:
                    chunks //= 2
                    i = pool.tensor_tensor(w[:, 0:chunks, :], w[:, 0:chunks, :], w[:, chunks:2 * chunks, :],
                                           ALU.add)
                    if chunks > 1:
                        own.mark(i)
                        own.wait()
                i.then_inc(folded, 1)

            def iteration(plan, b):
                prefetch = plan is not LAST
                if prefetch:
                    rstd(stats1_ready, b + 2, rstd1_ready, mv1, rstd1, slice(0, TT))
                if plan is FIRST:
                    fold_sizes(w1, C, 2)
                    fold_sizes(w2, FC, 4)
                for m in range(C):
                    for half in range(2):
                        lower_attn(b, m, half)
                for half in range(2):
                    rstd(stats2_ready, 2 * b + (half + 1), rstd2_ready, mv2, rstd2,
                         slice(TT // 2 * half, TT // 2 * (half + 1)))
                if prefetch:
                    k_diag_odd(plan, b, 0)
                wait_read(pool, plan, b, ("attn_out", TT - 1))
                if plan is FIRST:
                    wait_filled(pool, plan, b, "alpha2")
                add_row(x1_b2, x1[:, :, :], b2_row, x1_b2_ready)
                if prefetch:
                    k_diag_odd(plan, b, 1)
                    add_row(x_bo[:, :, :], x_in[:, :, :], bo_row, x_bo_ready)

            pool.memset(minus_half[:, :], -0.5)
            pool.memset(eps[:, :], EPS)
            pool.memset(ones[:, :], 1.0).then_inc(ones_ready, 1)
            pool.memset(v_ones[:, 0:UNITS // 2, :, :], 0.0).then_inc(zeros_ready, 1)
            pool.wait_ge(ones_ready, 1)
            rstd(stats1_ready, 1, rstd1_ready, mv1, rstd1, slice(0, TT))
            pool.memset(v_ones[:, UNITS // 2:, :, :], 0.0).then_inc(zeros_ready, 1)
            pool.wait_ge(const_loaded, 32)
            for m in range(C):
                k_diag_odd(START, 0, m)
            wait_read(pool, START, 0, "bias_out")
            add_row(x_bo[:, :, :], x_in[:, :, :], bo_row, x_bo_ready)
            iteration(FIRST, 0)
            before = own.n
            with pool.Fori(1, B - 1) as b:
                own.enter((b - 1) * 3 + before)
                iteration(LOOP, b)
                assert own.n == 3
            own.enter((B - 2) * 3 + before)
            iteration(LAST, B - 1)

        @block.scalar
        def _(act):
            def copy_norm1_t(plan, b, c):
                i = wait_filled(act, plan, b, ("norm1_t", c))
                act.activation(norm1_t[:, c, :], bank[i][:, :], ACT.Identity).then_inc(emptied[i], 1)

            def upper_norm1(plan, b, c):
                i = wait_filled(act, plan, b, ("norm1_t", c))
                act.activation(norm1_hi[:, c, :], bank[i][:, :], ACT.Identity).then_inc(norm1_hi_ready, 1)

            def upper_ctx(plan, b, c):
                if c == 0:
                    act.wait_ge(ctx_loaded, 16 * b + 32)
                    if plan is not FIRST:
                        for i in range(2):
                            wait_filled(act, *of_last_row(plan, b, ("ffn_out", i)))
                act.activation(ctx_hi[:, c, :], ctx_in[:, c, :], ACT.Identity).then_inc(ctx_hi_ready, 1)

            def project_bias(plan, b, kind, m):
                dst, bias = {"q": (q_dst, bq), "k": (k_dst, bk)}[kind]
                i = wait_filled(act, plan, b, (kind, m))
                act.activation(dst[m], bank[i][:, :], ACT.Identity, bias=bias[:, m:m + 1]).then_inc(emptied[i], 1)

            q_dst = [q_t[:, m, REACH:REACH + S] for m in range(C)]
            k_dst = [k_t[:, m, :] for m in range(C)]

            def exp_step(plan, b, t):
                act.wait_ge(shifted, b * STEPS + (t + 1))
                i, _ = uses_before(plan, b, ("scores", t))
                w = WIN * len(windows_of(t))
                act.activation(probs[:, t % 3, :, :].rearrange("p a b -> p (a b)")[:, 0:w],
                               bank[i][:, 0:w], ACT.Exp, scale=SCALE).then_inc(emptied[i], 1)

            def num_den(plan, b, u, half):
                m, r = u // 2, 64 * (u % 2)
                q = slice(HALF * half, HALF * (half + 1))
                i = wait_filled(act, plan, b, ("context", u))
                if u == 2:
                    act.wait_ge(ctx_raw_ready, 2 * C * b + (half + 1))
                act.activation(num[r:r + 64, m, q], bank[i][r:r + 64, q], ACT.Identity)
                act.activation(den[r:r + 64, q], bank[i][64 - r:128 - r, q],
                               ACT.Identity).then_inc(emptied[i] if half else half_read, 1)

            def upper_attn(b, m, half):
                act.wait_ge(ctx_raw_ready, 2 * C * b + (2 * m + half + 1))
                q = slice(HALF * half, HALF * (half + 1))
                act.activation(attn_hi[:, m, q], num[:, m, q], ACT.Identity).then_inc(attn_hi_ready, 1)

            def upper_norm2(plan, b, half):
                q = slice(HALF * half, HALF * (half + 1))
                for c in range(C):
                    i = wait_filled(act, plan, b, ("norm2_t", C * half + c))
                    act.activation(n2_hi[:, c, q], bank[i][:, 0:HALF], ACT.Identity).then_inc(n2_hi_ready, 1)

            def sign_or_size(n, size):
                if n == 0:
                    act.wait_ge(w12_loaded, 32)
                w = raw[:, C * F // 2 * n:C * F // 2 * (n + 1)]
                sign = (sign1, sign2)[n // 2][:, :, :].rearrange("p a b -> p (a b)")
                if size:
                    act.wait_ge(signs_ready, n + 1)
                    act.activation(w, w, ACT.Abs).then_inc(abs_ready, 1)
                else:
                    act.activation(sign[:, C * F // 2 * (n % 2):C * F // 2 * (n % 2 + 1)], w,
                                   ACT.Sign).then_inc(signs_ready, 1)

            def iteration(plan, b):
                prefetch = plan is not LAST
                for t in range(STEPS + 2):
                    if prefetch and t + AHEAD in T1_AT:
                        upper_norm1(plan, b, T1_AT.index(t + AHEAD))
                    if prefetch and t == STEPS - 4:
                        project_bias(plan, b, "k", 0)
                    if t < STEPS:
                        exp_step(plan, b, t)
                    for u in range(UNITS):
                        if t == last_step(u) + 2:
                            num_den(plan, b, u, 0)
                            num_den(plan, b, u, 1)
                    if plan is FIRST and 3 <= t < 7:
                        i = t - 3
                        if i == 3:
                            act.wait_ge(wo_loaded, 16)
                        act.activation(w_hi[:, i, :, :], (wq, wk, wv, wo)[i][:, :, :],
                                       ACT.Identity).then_inc(w_hi_ready, 1)
                    if t in (17, 18):
                        upper_attn(b, 0, t - 17)
                    if prefetch and t in (9, 10):
                        upper_ctx(plan, b, t - 9)
                    if plan is FIRST and 8 <= t < 16:
                        sign_or_size((t - 8) // 2, t % 2 == 1)
                    if plan is not FIRST and t == 6:
                        act.wait_ge(y_ready, b)
                        act.dma_start(tokens(out, (b - 1) * (S * D)), y[:, :, :]).then_inc(y_free, 16)
                if prefetch:
                    project_bias(plan, b, "q", 0)
                upper_attn(b, 1, 0)
                if prefetch:
                    project_bias(plan, b, "q", 1)
                    project_bias(plan, b, "k", 1)
                upper_attn(b, 1, 1)
                act.activation(wait_slot[:, 1:2], ones[:, 0:1], ACT.Gelu)
                upper_norm2(plan, b, 0)
                if prefetch:
                    upper_norm2(plan, b, 1)
                if plan is FIRST:
                    wait_read(act, plan, b, "alpha1")
                for n, i, q in hidden_pieces(plan is LAST):
                    if plan is LAST and n == SECOND_AT:
                        upper_norm2(plan, b, 1)
                    k, w = wait_filled(act, plan, b, ("hidden", n)), q.stop - q.start
                    act.activation(hid[:, n % 3, 0:w], bank[k][:, 0:w], ACT.Gelu, bias=b1[:, i:i + 1],
                                   scale=alpha1[:, i:i + 1]).then_inc(emptied[k], 1)
                    wait_read(act, plan, b, ("hidden", n))
                    act.activation(hid_hi[:, n % 3, 0:w], hid[:, n % 3, 0:w],
                                   ACT.Identity).then_inc(hid_hi_ready, 1)

            act.dma_start(wk[:, :, :], wk_t.rearrange("(c p) n -> p c n", p=P)).then_inc(wk_loaded, 16)
            act.dma_start(const[:, :], consts).then_inc(const_loaded, 16)
            act.dma_start(col[:, :], cols).then_inc(const_loaded, 16)
            act.wait_ge(ones_ready, 1)
            act.activation(wait_slot[:, 1:2], ones[:, 0:1], ACT.Exp)
            act.wait_ge(const_loaded, 32)
            for m in range(C):
                project_bias(START, 0, "k", m)
            for c in range(C):
                copy_norm1_t(START, 0, c)
            act.wait_ge(tables_ready, 1)
            for m in range(C):
                project_bias(START, 0, "q", m)
            act.sem_inc(y_free, 16)
            iteration(FIRST, 0)
            with act.Fori(1, B - 1) as b:
                iteration(LOOP, b)
            iteration(LAST, B - 1)

        @block.vector
        def _(dve):
            own = Own(dve, dve_done)

            def statistics(src, stats, mv, stats_ready, tiles):
                for t in tiles:
                    own.mark(dve.bn_stats(stats[:, t, :], src[:, t, :]))
                own.wait()
                dve.memset(wait_slot[:, 0:1], 0.0)
                for t in tiles:
                    i = dve.bn_aggr(mv[:, t, :], stats[:, t, :])
                i.then_inc(stats_ready, 1)

            def normalize(src, mv, rstd, dst, rstd_ready, made, ready, tiles):
                dve.wait_ge(rstd_ready, made)
                for t in tiles:
                    i = dve.tensor_scalar(dst[:, t, :], src[:, t, :], mv[:, t, 0:1], rstd[:, t:t + 1],
                                          ALU.subtract, ALU.mult)
                i.then_inc(ready, 1)

            def k_diag_even(plan, b, m, heads):
                wait_read(dve, plan, b, ("k", m))
                for p in heads:
                    i = dve.tensor_scalar(
                        k_diag[:, 2 * m, :, QB * p:QB * (p + 1)],
                        k_t[:, m, :].rearrange("r (j k) -> r j k", k=QB),
                        head_mask[:, 2 * p:2 * p + 1], None, ALU.mult)
                if HU - 1 in heads:
                    i.then_inc(k_diag_dve, 1)

            def v_transpose(plan, b, m):
                i = wait_filled(dve, plan, b, ("v", m))
                dve.transpose(v_t[:, m, :], bank[i][:, :]).then_inc(emptied[i], 1)

            def v_ones_set(m):
                dve.wait_ge(zeros_ready, m + 1)
                for u in (2 * m, 2 * m + 1):
                    dve.tensor_copy(part(v_ones[:, u, 0, 64 * (1 - u % 2):], 0, [P, NB], [DH, HU], [1, DH]),
                                    part(const[:, C_QUAD:], 0, [0, NB], [QB, HU], [0, DH]))

            def v_place(plan, b, m, heads):
                wait_read(dve, plan, b, ("v", m))
                for p in heads:
                    r = slice(QB * p, QB * (p + 1))
                    dst = v_ones[r, 2 * m, 0, DH * p:DH * (p + 1)]
                    i = dve.tensor_copy(
                        part(dst, 0, [NB * P + 64, 2], [P, NB], [1, DH]),
                        v_t[r, m, :].rearrange("k (j s d) -> k s j d", j=NB, s=2))
                if HU - 1 in heads:
                    i.then_inc(v_ready, 1)

            def step_max(plan, b, t, rows_on=0):
                i = wait_filled(dve, plan, b, (("scores", "scores of next")[rows_on], t))
                for u, j, n, slot in runs_of(t):
                    own.mark(dve.tensor_reduce(
                        part_max[:, u % 2, j + TPAD:j + TPAD + n, :].rearrange("p a b -> p (a b)"),
                        bank[i][:, WIN * slot:WIN * (slot + n)].rearrange("p (a b) -> p a b", b=QB),
                        AX.X, ALU.max, apply_transpose=True))
                own.wait()
                for u, i0, i1 in finished_blocks(t):
                    first = part_max[:, u % 2, i0, WB - 1:WB]
                    own.mark(dve.tensor_reduce(
                        neg_max[:, u % 2, i0:i1],
                        part(first, 0, [WB, i1 - i0], [WB - 1, WB]),
                        AX.X, ALU.max, negate=True))
                own.wait()
                for u, i0, i1 in finished_blocks(t):
                    n = i1 - i0
                    last = dve.tensor_tensor(
                        max_diag[:, u % 2, REACH + QB * i0:REACH + QB * i1].rearrange("p (a b) -> p a b", b=QB),
                        part(delta, 0, [0, n], [1, QB]),
                        part(neg_max[:, u % 2, i0:i1], 0, [1, n], [0, QB]), ALU.mult)
                last.then_inc(max_ready, 1)

            def reciprocal(q):
                own.mark(dve.reciprocal(den[:, q], den[:, q]))

            def divide(m, half):
                own.wait()
                q = slice(HALF * half, HALF * (half + 1))
                dve.tensor_tensor(num[:, m, q], num[:, m, q], den[:, q], ALU.mult).then_inc(ctx_raw_ready, 1)

            def wait_num_den(plan, b, m, half):
                if half:
                    wait_read(dve, plan, b, ("context", 2 * m))
                    wait_read(dve, plan, b, ("context", 2 * m + 1))
                else:
                    dve.wait_ge(half_read, UNITS * b + (2 * m + 2))

            def mean_size(plan, name, dst, count):
                i = wait_filled(dve, plan, 0, name)
                dve.tensor_scalar(dst[:, :], bank[i][:, 0:dst.shape[1]], 1.0 / count, None,
                                  ALU.mult).then_inc(emptied[i], 1)

            def residual(plan, b, i):
                k = wait_filled(dve, plan, b, ("attn_out", i))
                dve.tensor_tensor(x1[:, i, :], bank[k][:, 0:D], x_bo[:, i, :], ALU.add).then_inc(emptied[k], 1)

            def statistics2(plan, b, half):
                tiles = range(TT // 2 * half, TT // 2 * (half + 1))
                for i in tiles:
                    wait_read(dve, plan, b, ("attn_out", i))
                statistics(x1, stats2, mv2, stats2_ready, tiles)

            def lower_norm2(plan, b, half):
                q = slice(HALF * half, HALF * (half + 1))
                for c in range(C):
                    n = C * half + c
                    i, _ = uses_before(plan, b, ("norm2_t", n))
                    dve.wait_ge(n2_hi_ready, 2 * C * b + (n + 1))
                    dve.tensor_tensor(n2_lo[:, c, q], bank[i][:, 0:HALF], n2_hi[:, c, q].bitcast(F32),
                                      ALU.subtract).then_inc(emptied[i], 1)

            def scale_out(plan, b, i):
                k = wait_filled(dve, *of_last_row(plan, b, ("ffn_out", i)))
                dve.tensor_tensor(norm2[:, 2 * i:2 * i + 2, :], bank[k][:, :].rearrange("p (t d) -> p t d", d=D),
                                  part(alpha2[:, :], 0, [0, 2], [1, D]), ALU.mult).then_inc(emptied[k], 1)

            def finish_row(plan, b):
                for i in range(2):
                    wait_read(dve, *of_last_row(plan, b, ("ffn_out", i)))
                dve.wait_ge(x1_b2_ready, b)
                dve.wait_ge(y_free, 16 * b)
                dve.tensor_tensor(y[:, :, :], norm2[:, :, :], x1_b2[:, :, :], ALU.add).then_inc(y_ready, 1)

            def finish_half(i):
                t = slice(2 * i, 2 * i + 2)
                wait_read(dve, *of_last_row(LAST, B, ("ffn_out", i)))
                dve.wait_ge(x1_b2_ready, B)
                dve.wait_ge(y_free, 16 * B)
                dve.tensor_tensor(y[:, t, :], norm2[:, t, :], x1_b2[:, t, :], ALU.add).then_inc(y_ready, 1)

            def iteration(plan, b):
                prefetch = plan is not LAST
                recip_at = (last_step(1) + AHEAD + 3, last_step(1) + AHEAD + 5)
                if plan is not FIRST:
                    for i in range(2):
                        scale_out(plan, b, i)
                for t in range(AHEAD, STEPS):
                    step_max(plan, b, t)
                    if plan is not FIRST and t == 4:
                        finish_row(plan, b)
                    if prefetch and t == (8 if plan is FIRST else 5):
                        dve.wait_ge(x_loaded, 16 * b + 32)
                        statistics(x_in, stats1, mv1, stats1_ready, range(TT))
                    if prefetch and t == (10 if plan is FIRST else 7):
                        normalize(x_in, mv1, rstd1, norm1, rstd1_ready, b + 2, norm1_ready, range(TT))
                    if prefetch and t in T1_AT:
                        c = T1_AT.index(t)
                        i, _ = uses_before(plan, b, ("norm1_t", c))
                        dve.wait_ge(norm1_hi_ready, C * b + (c + 1))
                        dve.tensor_tensor(norm1_lo[:, c, :], bank[i][:, :], norm1_hi[:, c, :].bitcast(F32),
                                          ALU.subtract).then_inc(emptied[i], 1)
                    if prefetch and t in (14, 15):
                        c = t - 14
                        dve.wait_ge(ctx_hi_ready, C * b + (c + 1))
                        dve.tensor_tensor(ctx_lo[:, c, :], ctx_in[:, c, :], ctx_hi[:, c, :].bitcast(F32),
                                          ALU.subtract).then_inc(ctx_lo_ready, 1)
                    if plan is FIRST and 16 <= t < 20:
                        i = t - 16
                        dve.wait_ge(w_hi_ready, i + 1)
                        dve.tensor_tensor(w_lo[:, i, :, :], (wq, wk, wv, wo)[i][:, :, :],
                                          w_hi[:, i, :, :].bitcast(F32), ALU.subtract).then_inc(w_lo_ready, 1)
                    if plan is FIRST and t in (4, 5):
                        k_diag_even(START, 0, 1, range(2 * t - 8, 2 * t - 6))
                    if plan is FIRST and t == 6:
                        v_ones_set(1)
                    if plan is FIRST and t == 7:
                        v_place(START, 0, 1, range(HU))
                    for half in range(2):
                        for piece in range(2):
                            if t == recip_at[half] + piece:
                                if piece == 0:
                                    wait_num_den(plan, b, 0, half)
                                q0 = HALF * half + HALF // 2 * piece
                                reciprocal(slice(q0, q0 + HALF // 2))
                                if piece == 1:
                                    divide(0, half)
                if prefetch:
                    k_diag_even(plan, b, 0, range(HU))
                for half in range(2):
                    wait_num_den(plan, b, 1, half)
                    reciprocal(slice(HALF * half, HALF * (half + 1)))
                    divide(1, half)
                dve.wait_ge(x_bo_ready, b + 1)
                halves = (range(TT // 2), range(TT // 2, TT))
                if plan is FIRST:
                    mean_size(plan, "alpha1", alpha1, D)
                for i in halves[0]:
                    residual(plan, b, i)
                statistics2(plan, b, 0)
                if prefetch:
                    v_transpose(plan, b, 0)
                for i in halves[1]:
                    residual(plan, b, i)
                normalize(x1, mv2, rstd2, norm2, rstd2_ready, 2 * b + 1, norm2_ready, halves[0])
                statistics2(plan, b, 1)
                if prefetch:
                    v_transpose(plan, b, 1)
                lower_norm2(plan, b, 0)
                normalize(x1, mv2, rstd2, norm2, rstd2_ready, 2 * b + 2, norm2_ready, halves[1])
                if plan is FIRST:
                    mean_size(plan, "alpha2", alpha2, F)
                if prefetch:
                    lower_norm2(plan, b, 1)
                for n, _, q in hidden_pieces(plan is LAST):
                    if prefetch:
                        heads = range(0, 2) if n in (3, 6) else range(2, HU)
                        if n < AHEAD:
                            step_max(plan, b, n, 1)
                        elif n < 5:
                            v_place(plan, b, 0, heads)
                        elif n == 5:
                            k_diag_even(plan, b, 1, range(HU))
                        else:
                            v_place(plan, b, 1, heads)
                    if plan is LAST and n == SECOND_AT:
                        lower_norm2(plan, b, 1)
                    if plan is LAST and n == FC + 3:
                        scale_out(LAST, B, 0)
                    if plan is LAST and n == FC + 4:
                        finish_half(0)
                    w = q.stop - q.start
                    dve.wait_ge(hid_hi_ready, b * FC + (n + 1))
                    dve.tensor_tensor(hid_lo[:, n % 3, 0:w], hid[:, n % 3, 0:w],
                                      hid_hi[:, n % 3, 0:w].bitcast(F32),
                                      ALU.subtract).then_inc(hid_lo_ready, 1)
                if plan is LAST:
                    scale_out(LAST, B, 1)
                    finish_half(1)

            dve.memset(part_max[:, :, :, :], -BIG)
            dve.memset(max_diag[:, :, :].bitcast(F32), 0.0)
            dve.memset(q_t[:, :, 0:REACH], 0.0)
            dve.memset(q_t[:, :, REACH + S:], 0.0)
            dve.wait_ge(x_loaded, 16)
            statistics(x_in, stats1, mv1, stats1_ready, range(TT))
            dve.wait_ge(const_loaded, 32)
            dve.tensor_copy(quad_ones[:, :], const[:, C_QUAD:C_QUAD + P])
            dve.tensor_copy(ident16[:, :], ident)
            dve.tensor_copy(edge16[:, :, :].rearrange("p a b -> p (a b)"),
                            const[:, C_EDGE:C_END]).then_inc(tables_ready, 1)
            normalize(x_in, mv1, rstd1, norm1, rstd1_ready, 1, norm1_ready, range(TT))
            k_diag_even(START, 0, 0, range(HU))
            v_transpose(START, 0, 0)
            v_ones_set(0)
            v_transpose(START, 0, 1)
            v_place(START, 0, 0, range(HU))
            dve.wait_ge(wo_loaded, 16)
            for m in range(C):
                i = dve.tensor_scalar(norm2[:, m, :], wo[:, m, :], bv[:, m:m + 1], None, ALU.mult)
            i.then_inc(bv_wo_ready, 1)
            for t in range(AHEAD):
                step_max(START, -1, t, 1)
            i = wait_filled(dve, START, 0, "bias_out")
            dve.wait_ge(rows_loaded, 32)
            dve.tensor_tensor(bo_row[:, :], bank[i][:, 0:D], bo_row[:, :], ALU.add).then_inc(emptied[i], 1)
            iteration(FIRST, 0)
            before = own.n
            with dve.Fori(1, B - 1) as b:
                own.enter((b - 1) * DVE_OWN + before)
                iteration(LOOP, b)
                assert own.n == DVE_OWN, own.n
            own.enter((B - 2) * DVE_OWN + before)
            iteration(LAST, B - 1)

        @block.tensor
        def _(pe):
            def take(plan, b, name):
                i, before = uses_before(plan, b, name)
                if not (isinstance(before, int) and before == 0):
                    pe.wait_ge(emptied[i], before)
                return i

            def keep_busy(n):
                for _ in range(n):
                    pe.matmul(bank[2][:, 0:P], ones[:, :], ones[:, :], start=True, stop=True)

            def transpose_norm(plan, b, name, src, c, tiles):
                i = take(plan, b, name)
                for k, t in enumerate(tiles):
                    ins = pe.transpose(bank[i][:, P * k:P * (k + 1)], src[:, t, P * c:P * (c + 1)], ident)
                ins.then_inc(filled[i], 1)

            def transpose_norm2(plan, b, half):
                pe.wait_ge(norm2_ready, 2 * b + (half + 1))
                for c in range(C):
                    transpose_norm(plan, b, ("norm2_t", C * half + c), norm2, c,
                                   range(TT // 2 * half, TT // 2 * (half + 1)))

            def project(plan, b, kind, m):
                i = take(plan, b, (kind, m))
                half = slice(P * m, P * (m + 1))
                if plan is START:
                    w, src = {"q": (wq, norm1_t), "k": (wk, ctx_in), "v": (wv, ctx_in)}[kind]
                    passes = [(w[:, c, half], src[:, c, :]) for c in range(C)]
                else:
                    n = ("q", "k", "v").index(kind)
                    hi, lo = (norm1_hi, norm1_lo) if kind == "q" else (ctx_hi, ctx_lo)
                    passes = [(w[:, n, c, half], src[:, c, :]) for c in range(C)
                              for w, src in ((w_hi, hi), (w_lo, hi), (w_hi, lo))]
                for k, (w, src) in enumerate(passes):
                    ins = pe.matmul(bank[i][:, :], w, src, start=(k == 0), stop=(k == len(passes) - 1))
                ins.then_inc(filled[i], 1)

            def scores(plan, b, t, rows_on=0):
                i = take(plan, b, (("scores", "scores of next")[rows_on], t))
                b = b + rows_on
                n = len(windows_of(t))
                pe.matmul(part(bank[i][:, 0:1], 0, [WIN, n], [WIN - QB, 2], [1, QB]), ident16[:, :],
                          part(edge16[:, 0, 0:1], 0, [0, n], [QB, 2], [1, QB]),
                          start=True, stop=False, skip_group_check=True)
                for u, j, slot in windows_of(t):
                    if j == 0 and u % 2 == 0:
                        pe.wait_ge(k_diag_dve, C * b + (u // 2 + 1))
                    if j == 0 and u % 2 == 1:
                        pe.wait_ge(k_diag_pool, C * b + (u // 2 + 1))
                    w0 = 1 if j < TPAD else 0
                    w1_ = WB - 1 if j >= NB - TPAD else WB
                    ins = pe.matmul(bank[i][:, WIN * slot + QB * w0:WIN * slot + QB * w1_],
                                    k_diag[:, u, j, :], q_t[:, u // 2, QB * (j + w0):QB * (j + w1_)],
                                    start=False, stop=False, skip_group_check=True)
                ins.then_inc(filled[i], 1)

            def shift(plan, b, t):
                i, _ = uses_before(plan, b, ("scores", t))
                u, j, _ = windows_of(t)[-1]
                last = NB * u + min(j + 2 * TPAD, NB - 1)
                pe.wait_ge(max_ready, b * STEPS + (last // PER_BANK + 1))
                for u, j, n, slot in runs_of(t):
                    ins = pe.matmul(bank[i][:, WIN * slot:WIN * (slot + n)], quad_ones[:, :],
                                    part(max_diag[:, u % 2, QB * j:QB * j + 1], 0, [QB, n], [1, WIN]),
                                    start=False, stop=True, skip_group_check=True)
                ins.then_inc(shifted, 1)

            def context(plan, b, t):
                wait_read(pe, plan, b, ("scores", t))
                for u, j, slot in windows_of(t):
                    if j == 0:
                        take(plan, b, ("context", u))
                        pe.wait_ge(v_ready, C * b + (u // 2 + 1))
                    i, _ = uses_before(plan, b, ("context", u))
                    i0, i1 = max(0, j - TPAD), min(NB, j + TPAD + 1)
                    w0 = i0 - j + TPAD
                    ins = pe.matmul(bank[i][:, QB * i0:QB * i1], v_ones[:, u, j, :],
                                    probs[:, t % 3, slot, QB * w0:QB * (w0 + i1 - i0)],
                                    start=(j == 0), stop=(j == NB - 1), skip_group_check=True)
                    if j == NB - 1:
                        ins.then_inc(filled[i], 1)

            def attention_out(plan, b, i):
                k = take(plan, b, ("attn_out", i))
                done = 2 * C * b + (2 * C - 1 + i // (TT // 2))
                for m in range(C):
                    for attn, w in ((attn_hi, w_hi), (attn_hi, w_lo), (attn_lo, w_hi)):
                        if m == C - 1:
                            pe.wait_ge(attn_hi_ready if attn is attn_hi else attn_ready, done)
                        ins = pe.matmul(bank[k][:, 0:D], attn[:, m, P * i:P * (i + 1)], w[:, 3, m, :],
                                        start=(m == 0 and attn is attn_hi and w is w_hi),
                                        stop=(m == C - 1 and attn is attn_lo))
                ins.then_inc(filled[k], 1)

            def sums_of_sizes(plan, which):
                k = take(plan, 0, which)
                if which == "alpha1":
                    pe.wait_ge(folded, 1)
                    for i in range(FC):
                        ins = pe.matmul(bank[k][:, i:i + 1], w1[:, 0, P * i:P * (i + 1)], ones[:, 0:1],
                                        start=True, stop=True)
                else:
                    pe.wait_ge(folded, 2)
                    ins = pe.matmul(bank[k][:, 0:D], ones[:, :], w2[:, 0, :], start=True, stop=True)
                ins.then_inc(filled[k], 1)

            def hidden(plan, b, n, i, q):
                k, w = take(plan, b, ("hidden", n)), q.stop - q.start
                for side in (n2_hi, n2_lo):
                    for c in range(C):
                        if i == 0:
                            m = C * (q.stop // HALF - 1) + c
                            if side is n2_hi:
                                pe.wait_ge(n2_hi_ready, 2 * C * b + (m + 1))
                            else:
                                wait_read(pe, plan, b, ("norm2_t", m))
                        ins = pe.matmul(bank[k][:, 0:w], sign1[:, c, P * i:P * (i + 1)], side[:, c, q],
                                        start=(c == 0 and side is n2_hi),
                                        stop=(c == C - 1 and side is n2_lo))
                ins.then_inc(filled[k], 1)

            def ffn_out(plan, b, n, i, q):
                for side in (hid_hi, hid_lo):
                    pe.wait_ge(hid_hi_ready if side is hid_hi else hid_lo_ready, b * FC + (n + 1))
                    for t in range(q.start // P, q.stop // P):
                        k, _ = uses_before(plan, b, ("ffn_out", t // 2))
                        if i == 0 and t % 2 == 0 and side is hid_hi:
                            take(plan, b, ("ffn_out", t // 2))
                        ins = pe.matmul(bank[k][:, D * (t % 2):D * (t % 2 + 1)],
                                        side[:, n % 3, P * t - q.start:P * (t + 1) - q.start],
                                        sign2[:, i, :], start=(i == 0 and t % 2 == 0 and side is hid_hi),
                                        stop=(i == FC - 1 and side is hid_lo), skip_group_check=True)
                        if i == FC - 1 and t % 2 and side is hid_lo:
                            ins.then_inc(filled[k], 1)

            def iteration(plan, b):
                prefetch = plan is not LAST
                for t in range(AHEAD, STEPS):
                    scores(plan, b, t)
                    if prefetch and t in T1_AT:
                        if t == T1_AT[0]:
                            pe.wait_ge(norm1_ready, b + 2)
                        transpose_norm(plan, b, ("norm1_t", T1_AT.index(t)), norm1, T1_AT.index(t), range(TT))
                    if prefetch and t == STEPS - 1:
                        if plan is FIRST:
                            pe.wait_ge(w_lo_ready, 4)
                        pe.wait_ge(ctx_lo_ready, C * b + C)
                        project(plan, b, "k", 0)
                    if t > AHEAD:
                        context(plan, b, t - AHEAD - 1)
                    shift(plan, b, t - AHEAD)
                shift(plan, b, STEPS - 3)
                shift(plan, b, STEPS - 2)
                context(plan, b, STEPS - 4)
                shift(plan, b, STEPS - 1)
                for t in range(STEPS - 3, STEPS):
                    context(plan, b, t)
                if prefetch:
                    for c in range(C):
                        wait_read(pe, plan, b, ("norm1_t", c))
                    for m in range(C):
                        project(plan, b, "q", m)
                    project(plan, b, "k", 1)
                else:
                    keep_busy(14)
                if plan is FIRST:
                    sums_of_sizes(plan, "alpha1")
                pe.wait_ge(attn_ready, 2 * C * b + 2 * (C - 1))
                attention_out(plan, b, 0)
                attention_out(plan, b, 1)
                if prefetch:
                    project(plan, b, "v", 0)
                attention_out(plan, b, 2)
                attention_out(plan, b, 3)
                if prefetch:
                    project(plan, b, "v", 1)
                    scores(plan, b, 0, 1)
                else:
                    keep_busy(5)
                if plan is FIRST:
                    sums_of_sizes(plan, "alpha2")
                transpose_norm2(plan, b, 0)
                if prefetch:
                    for t in range(1, AHEAD):
                        scores(plan, b, t, 1)
                    transpose_norm2(plan, b, 1)
                pieces = hidden_pieces(plan is LAST)
                for k in range(len(pieces) + 2):
                    if plan is LAST and k == SECOND_AT:
                        transpose_norm2(plan, b, 1)
                    if k < len(pieces):
                        hidden(plan, b, *pieces[k])
                    if k >= 2:
                        ffn_out(plan, b, *pieces[k - 2])

            pe.wait_ge(ones_ready, 1)
            keep_busy(9)
            pe.wait_ge(ctx_loaded, 16)
            pe.wait_ge(wk_loaded, 16)
            for m in range(C):
                project(START, 0, "k", m)
            pe.wait_ge(wv_loaded, 16)
            project(START, 0, "v", 0)
            pe.wait_ge(const_loaded, 32)
            pe.wait_ge(norm1_ready, 1)
            for c in range(C):
                transpose_norm(START, 0, ("norm1_t", c), norm1, c, range(TT))
            project(START, 0, "v", 1)
            for c in range(C):
                wait_read(pe, START, 0, ("norm1_t", c))
            pe.wait_ge(wq_loaded, 16)
            for m in range(C):
                project(START, 0, "q", m)
            wait_read(pe, START, 0, ("q", 0))
            pe.wait_ge(tables_ready, 1)
            for t in range(AHEAD):
                scores(START, -1, t, 1)
            wait_read(pe, START, 0, ("q", 1))
            i = take(START, 0, "bias_out")
            pe.wait_ge(bv_wo_ready, 1)
            for m in range(C):
                ins = pe.matmul(bank[i][:, 0:D], ones[:, :], norm2[:, m, :], start=(m == 0), stop=(m == C - 1))
            ins.then_inc(filled[i], 1)
            iteration(FIRST, 0)
            with pe.Fori(1, B - 1) as b:
                iteration(LOOP, b)
            iteration(LAST, B - 1)


def kernel(x, ctx_1024, L0_xattn_Wq, L0_xattn_bq, L0_xattn_Wk, L0_xattn_bk, L0_xattn_Wv, L0_xattn_bv,
           L0_xattn_Wo, L0_xattn_bo, L0_ffn_w1, L0_ffn_b1, L0_ffn_w2, L0_ffn_b2):
    import numpy as np
    import concourse.bacc as bacc
    from concourse.bass_utils import run_bass_kernel_spmd

    def t(a):
        return np.ascontiguousarray(np.asarray(a).T)

    def by_unit(a):
        a = np.asarray(a)
        shape = a.shape
        return np.ascontiguousarray(a.reshape(C, HU, 2, DH, -1).transpose(0, 2, 1, 3, 4).reshape(shape))

    def columns(a):
        return np.asarray(a).reshape(-1, P).T

    r = np.arange(P)
    k, q = r[:, None] % QB, np.arange(QB)[None, :]
    consts = np.concatenate([
        np.eye(P), r[:, None] // QB == r[None, :] // QB, r[:, None] // DH == np.arange(2 * HU)[None, :],
        k == q, np.where(k > q, -BIG, 0.0), np.where(q > k, -BIG, 0.0)], axis=1).astype(np.float32)

    arrays = {
        "x": np.ascontiguousarray(np.asarray(x)),
        "ctx_t": np.ascontiguousarray(np.asarray(ctx_1024).transpose(0, 2, 1)),
        "wq_t": t(L0_xattn_Wq), "wk_t": t(L0_xattn_Wk), "wv_t": t(L0_xattn_Wv),
        "wo_t": by_unit(t(L0_xattn_Wo)),
        "w1_t": t(L0_ffn_w1), "w2_t": t(L0_ffn_w2),
        "cols": np.ascontiguousarray(np.concatenate(
            [columns(L0_xattn_bq), columns(L0_xattn_bk), columns(by_unit(L0_xattn_bv)),
             columns(L0_ffn_b1)], axis=1)),
        "rows": np.stack([np.asarray(L0_xattn_bo), np.asarray(L0_ffn_b2)]),
        "consts": consts,
    }
    nc = bacc.Bacc("TRN2", target_bir_lowering=False, num_devices=1)
    args = [nc.dram_tensor(name, a.shape, mybir.dt.from_np(a.dtype), kind="ExternalInput").ap()
            for name, a in arrays.items()]
    out = nc.dram_tensor("y_out", (B, S, D), F32, kind="ExternalOutput").ap()
    xattn_ffn_kernel(nc, *args, out)
    r = run_bass_kernel_spmd(nc, [arrays], core_ids=[0])
    return r.results[0]["y_out"]
```
